# Optimizing a Trainium2 kernel written in Bass

```python
import numpy as np
import jax
import jax.numpy as jnp

def _softmax(x, axis=-1):
    return jax.nn.softmax(x, axis=axis)

def _gelu(x):
    return jax.nn.gelu(x, approximate=True)

def _silu(x):
    return jax.nn.silu(x)

def _sigmoid(x):
    return jax.nn.sigmoid(x)

def _layernorm(x, axis=-1, eps=1e-05):
    m = jnp.mean(x, axis=axis, keepdims=True)
    v = jnp.var(x, axis=axis, keepdims=True)
    return (x - m) / jnp.sqrt(v + eps)

def _scatter_add(tgt, idx, src, axis=0):
    return tgt.at[idx].add(src)

def _segment_sum(src, seg, n):
    return jax.ops.segment_sum(src, seg, n)
kernel_name = 'mk_gnn_resnorm_d4_gnn_r64_aaf8e8'

def setup_inputs(seed: int=0):
    np.random.seed(seed)
    _w = jnp.asarray

    def _rec_inputs():
        import jax
        import jax.numpy as jnp
        _gk = jax.random.key(seed)
        x = -0.000202 + 1 * jax.random.normal(jax.random.fold_in(_gk, 1), (100000, 64), jnp.float32)
        src = jax.random.randint(jax.random.fold_in(_gk, 2), (25000,), 0, 100000, jnp.int32)
        dst = jnp.minimum((100000 * jax.random.uniform(jax.random.fold_in(_gk, 3), (25000,)) ** 2.0).astype(jnp.int32), 99999)
        _o = jnp.argsort(dst, stable=True)
        src = src[_o]
        dst = dst[_o]
        edge_attr_64 = -2.25437e-05 + 0.999858 * jax.random.normal(jax.random.fold_in(_gk, 12), (25000, 64), jnp.float32)
        edge_weight1 = 0.000452788 + 0.999756 * jax.random.normal(jax.random.fold_in(_gk, 15), (25000, 1), jnp.float32)
        return (x, src, dst, edge_attr_64, edge_weight1)
    x, src, dst, edge_attr_64, edge_weight1 = _rec_inputs()

    def _L0_gnn_setup():
        import jax, jax.numpy as jnp
        import numpy as np
        N = 100000
        E = 25000
        ND = 64
        ED = 1
        HD = 128
        key = jax.random.key(seed)
        ks = jax.random.split(key, 12)
        x = jax.random.normal(ks[0], (N, ND), dtype=jnp.float32)
        edge_index = jax.random.randint(ks[1], (2, E), 0, N, dtype=jnp.int32)
        edge_attr = jax.random.normal(ks[2], (E, ED), dtype=jnp.float32)
        s1 = 1.0 / np.sqrt(2 * ND + ED)
        W1 = jax.random.uniform(ks[3], (HD, 2 * ND + ED), minval=-s1, maxval=s1, dtype=jnp.float32)
        b1 = jax.random.uniform(ks[4], (HD,), minval=-s1, maxval=s1, dtype=jnp.float32)
        s2 = 1.0 / np.sqrt(HD)
        W2 = jax.random.uniform(ks[5], (ND, HD), minval=-s2, maxval=s2, dtype=jnp.float32)
        b2 = jax.random.uniform(ks[6], (ND,), minval=-s2, maxval=s2, dtype=jnp.float32)
        sg = 1.0 / np.sqrt(ND)
        W_ih = jax.random.uniform(ks[7], (3 * ND, ND), minval=-sg, maxval=sg, dtype=jnp.float32)
        b_ih = jax.random.uniform(ks[8], (3 * ND,), minval=-sg, maxval=sg, dtype=jnp.float32)
        W_hh = jax.random.uniform(ks[9], (3 * ND, ND), minval=-sg, maxval=sg, dtype=jnp.float32)
        b_hh = jax.random.uniform(ks[10], (3 * ND,), minval=-sg, maxval=sg, dtype=jnp.float32)
        return {'x': x, 'edge_index': edge_index, 'edge_attr': edge_attr, 'W1': W1, 'b1': b1, 'W2': W2, 'b2': b2, 'W_ih': W_ih, 'b_ih': b_ih, 'W_hh': W_hh, 'b_hh': b_hh}
    _L0_gnn_all = _L0_gnn_setup()
    _L0_gnn_in = {k: v for k, v in _L0_gnn_all.items() if k in ('W1', 'b1', 'W2', 'b2', 'W_ih', 'b_ih', 'W_hh', 'b_hh')}
    del _L0_gnn_all

    def _L1_gnn_setup():
        import jax, jax.numpy as jnp
        import numpy as np
        V = 100000
        E = 15625
        D = 64

        def gather_scatter(x, edges, directed=False):
            out = jnp.zeros_like(x)
            out = out.at[edges[:, 0]].add(x[edges[:, 1]])
            if not directed:
                out = out.at[edges[:, 1]].add(x[edges[:, 0]])
            return out
        key = jax.random.key(seed)
        k1, k2, k3, k4 = jax.random.split(key, 4)
        verts = jax.random.normal(k1, (V, D), dtype=jnp.float32)
        edges = jax.random.randint(k2, (E, 2), 0, V, dtype=jnp.int64)
        w0_w = jax.random.normal(k3, (D, D), dtype=jnp.float32) * 0.01
        w1_w = jax.random.normal(k4, (D, D), dtype=jnp.float32) * 0.01
        w0_b = jnp.zeros((D,), dtype=jnp.float32)
        w1_b = jnp.zeros((D,), dtype=jnp.float32)
        return {'verts': verts, 'edges': edges, 'w0_w': w0_w, 'w0_b': w0_b, 'w1_w': w1_w, 'w1_b': w1_b}
    _L1_gnn_all = _L1_gnn_setup()
    _L1_gnn_in = {k: v for k, v in _L1_gnn_all.items() if k in ('w0_w', 'w0_b', 'w1_w', 'w1_b')}
    del _L1_gnn_all

    def _L2_gnn_setup():
        import jax, jax.numpy as jnp
        import numpy as np
        N_NODES = 100000
        N_EDGES = 25000
        IN_DIM = 64
        OUT_DIM = 64
        key = jax.random.key(seed)
        k_x, k_e, k_wm, k_bm, k_wu, k_bu = jax.random.split(key, 6)
        x = jax.random.normal(k_x, (N_NODES, IN_DIM), dtype=jnp.float32)
        edge_index = jax.random.randint(k_e, (2, N_EDGES), 0, N_NODES, dtype=jnp.int64)
        lim_m = 1.0 / np.sqrt(2 * IN_DIM)
        lim_u = 1.0 / np.sqrt(IN_DIM + OUT_DIM)
        W_msg = jax.random.uniform(k_wm, (2 * IN_DIM, OUT_DIM), jnp.float32, -lim_m, lim_m)
        b_msg = jax.random.uniform(k_bm, (OUT_DIM,), jnp.float32, -lim_m, lim_m)
        W_upd = jax.random.uniform(k_wu, (IN_DIM + OUT_DIM, OUT_DIM), jnp.float32, -lim_u, lim_u)
        b_upd = jax.random.uniform(k_bu, (OUT_DIM,), jnp.float32, -lim_u, lim_u)
        return {'x': x, 'edge_index': edge_index, 'W_msg': W_msg, 'b_msg': b_msg, 'W_upd': W_upd, 'b_upd': b_upd}
    _L2_gnn_all = _L2_gnn_setup()
    _L2_gnn_in = {k: v for k, v in _L2_gnn_all.items() if k in ('W_msg', 'b_msg', 'W_upd', 'b_upd')}
    del _L2_gnn_all

    def _L3_gnn_setup():
        import jax, jax.numpy as jnp
        import numpy as np
        N_NODES = 100000
        N_EDGES = 15625
        D_NODE = 64
        D_EDGE = 64
        key = jax.random.key(seed)
        ks = jax.random.split(key, 8)
        node_features = jax.random.normal(ks[0], (N_NODES, D_NODE), dtype=jnp.float32)
        edge_features = jax.random.normal(ks[1], (N_EDGES, D_EDGE), dtype=jnp.float32)
        src = jax.random.randint(ks[2], (N_EDGES,), 0, N_NODES)
        tgt = jax.random.randint(ks[3], (N_EDGES,), 0, N_NODES)
        fan_msg = D_NODE + D_EDGE
        W_msg = jax.random.uniform(ks[4], (fan_msg, D_NODE), dtype=jnp.float32, minval=-1.0 / np.sqrt(fan_msg), maxval=1.0 / np.sqrt(fan_msg))
        b_msg = jnp.zeros((D_NODE,), dtype=jnp.float32)
        W_upd = jax.random.uniform(ks[5], (D_NODE, D_NODE), dtype=jnp.float32, minval=-1.0 / np.sqrt(D_NODE), maxval=1.0 / np.sqrt(D_NODE))
        b_upd = jnp.zeros((D_NODE,), dtype=jnp.float32)
        eps = jnp.zeros((1,), dtype=jnp.float32)
        return {'node_features': node_features, 'edge_features': edge_features, 'W_msg': W_msg, 'b_msg': b_msg, 'W_upd': W_upd, 'b_upd': b_upd, 'eps': eps, 'src': src, 'tgt': tgt}
    _L3_gnn_all = _L3_gnn_setup()
    _L3_gnn_in = {k: v for k, v in _L3_gnn_all.items() if k in ('W_msg', 'b_msg', 'W_upd', 'b_upd', 'eps')}
    del _L3_gnn_all
    return {'x': x, 'src': src, 'dst': dst, 'edge_attr_64': edge_attr_64, 'edge_weight1': edge_weight1, 'L0_gnn_W1': _L0_gnn_in['W1'], 'L0_gnn_b1': _L0_gnn_in['b1'], 'L0_gnn_W2': _L0_gnn_in['W2'], 'L0_gnn_b2': _L0_gnn_in['b2'], 'L0_gnn_W_ih': _L0_gnn_in['W_ih'], 'L0_gnn_b_ih': _L0_gnn_in['b_ih'], 'L0_gnn_W_hh': _L0_gnn_in['W_hh'], 'L0_gnn_b_hh': _L0_gnn_in['b_hh'], 'L1_gnn_w0_w': _L1_gnn_in['w0_w'], 'L1_gnn_w0_b': _L1_gnn_in['w0_b'], 'L1_gnn_w1_w': _L1_gnn_in['w1_w'], 'L1_gnn_w1_b': _L1_gnn_in['w1_b'], 'L2_gnn_W_msg': _L2_gnn_in['W_msg'], 'L2_gnn_b_msg': _L2_gnn_in['b_msg'], 'L2_gnn_W_upd': _L2_gnn_in['W_upd'], 'L2_gnn_b_upd': _L2_gnn_in['b_upd'], 'L3_gnn_W_msg': _L3_gnn_in['W_msg'], 'L3_gnn_b_msg': _L3_gnn_in['b_msg'], 'L3_gnn_W_upd': _L3_gnn_in['W_upd'], 'L3_gnn_b_upd': _L3_gnn_in['b_upd'], 'L3_gnn_eps': _L3_gnn_in['eps']}

def reference(x, src, dst, edge_attr_64, edge_weight1, L0_gnn_W1, L0_gnn_b1, L0_gnn_W2, L0_gnn_b2, L0_gnn_W_ih, L0_gnn_b_ih, L0_gnn_W_hh, L0_gnn_b_hh, L1_gnn_w0_w, L1_gnn_w0_b, L1_gnn_w1_w, L1_gnn_w1_b, L2_gnn_W_msg, L2_gnn_b_msg, L2_gnn_W_upd, L2_gnn_b_upd, L3_gnn_W_msg, L3_gnn_b_msg, L3_gnn_W_upd, L3_gnn_b_upd, L3_gnn_eps):
    import jax
    import jax.numpy as jnp

    def _L0_gnn_ref(x, edge_index, edge_attr, W1, b1, W2, b2, W_ih, b_ih, W_hh, b_hh):
        import jax, jax.numpy as jnp
        import numpy as np
        N = 100000
        E = 25000
        ND = 64
        ED = 1
        HD = 128
        src, dst = (edge_index[0], edge_index[1])
        m = jnp.concatenate([x[src], x[dst], edge_attr], axis=-1)
        m = jax.nn.relu(m @ W1.T + b1) @ W2.T + b2
        aggr = jnp.zeros_like(x).at[dst].add(m)
        gi = aggr @ W_ih.T + b_ih
        gh = x @ W_hh.T + b_hh
        i_r, i_z, i_n = jnp.split(gi, 3, axis=-1)
        h_r, h_z, h_n = jnp.split(gh, 3, axis=-1)
        r = jax.nn.sigmoid(i_r + h_r)
        z = jax.nn.sigmoid(i_z + h_z)
        n = jnp.tanh(i_n + r * h_n)
        return (1.0 - z) * n + z * x

    def _L1_gnn_ref(verts, edges, w0_w, w0_b, w1_w, w1_b):
        import jax, jax.numpy as jnp
        import numpy as np
        V = 100000
        E = 15625
        D = 64

        def gather_scatter(x, edges, directed=False):
            out = jnp.zeros_like(x)
            out = out.at[edges[:, 0]].add(x[edges[:, 1]])
            if not directed:
                out = out.at[edges[:, 1]].add(x[edges[:, 0]])
            return out
        verts_w0 = verts @ w0_w.T + w0_b
        verts_w1 = verts @ w1_w.T + w1_b
        neighbor_sums = gather_scatter(verts_w1, edges, directed=False)
        return verts_w0 + neighbor_sums

    def _L2_gnn_ref(x, edge_index, W_msg, b_msg, W_upd, b_upd):
        import jax, jax.numpy as jnp
        import numpy as np
        N_NODES = 100000
        N_EDGES = 25000
        IN_DIM = 64
        OUT_DIM = 64
        num_nodes = x.shape[0]
        source, target = (edge_index[0], edge_index[1])
        edge_feats = jnp.concatenate([x[source], x[target]], axis=-1)
        messages = jax.nn.relu(edge_feats @ W_msg + b_msg)
        agg_sum = jax.ops.segment_sum(messages, target, num_segments=num_nodes)
        counts = jax.ops.segment_sum(jnp.ones_like(target, dtype=x.dtype), target, num_segments=num_nodes)
        aggregated = agg_sum / jnp.clip(counts, 1.0, None)[:, None]
        updated = jax.nn.relu(jnp.concatenate([x, aggregated], axis=-1) @ W_upd + b_upd)
        return updated

    def _L3_gnn_ref(node_features, edge_features, W_msg, b_msg, W_upd, b_upd, eps, src, tgt):
        import jax, jax.numpy as jnp
        import numpy as np
        N_NODES = 100000
        N_EDGES = 15625
        D_NODE = 64
        D_EDGE = 64
        src_feats = node_features[src]
        msg_in = jnp.concatenate([src_feats, edge_features], axis=-1)
        messages = jax.nn.gelu(msg_in @ W_msg + b_msg)
        agg = jax.ops.segment_sum(messages, tgt, num_segments=node_features.shape[0])
        h = (1.0 + eps) * node_features + agg
        out = jax.nn.gelu(h @ W_upd + b_upd)
        return out
    edge_index = jnp.stack([src, dst])
    edge_index_t = jnp.stack([src, dst], axis=1)
    x = _layernorm(x + _L0_gnn_ref(x, edge_index, edge_weight1, L0_gnn_W1, L0_gnn_b1, L0_gnn_W2, L0_gnn_b2, L0_gnn_W_ih, L0_gnn_b_ih, L0_gnn_W_hh, L0_gnn_b_hh), axis=-1)
    x = _layernorm(x + _L1_gnn_ref(x, edge_index_t, L1_gnn_w0_w, L1_gnn_w0_b, L1_gnn_w1_w, L1_gnn_w1_b), axis=-1)
    x = _layernorm(x + _L2_gnn_ref(x, edge_index, L2_gnn_W_msg, L2_gnn_b_msg, L2_gnn_W_upd, L2_gnn_b_upd), axis=-1)
    x = _layernorm(x + _L3_gnn_ref(x, edge_attr_64, L3_gnn_W_msg, L3_gnn_b_msg, L3_gnn_W_upd, L3_gnn_b_upd, L3_gnn_eps, src, dst), axis=-1)
    return x

_drawn_inputs = setup_inputs


def setup_inputs(seed=0):
    import zlib

    import numpy as np

    out = dict(_drawn_inputs(seed))
    spreads = {'L1_gnn_w0_b': (0.0, 0.1),
     'L1_gnn_w1_b': (0.0, 0.1),
     'L3_gnn_b_msg': (0.0, 0.752),
     'L3_gnn_b_upd': (0.0, 0.1)}
    factors = {'edge_weight1': 8.0,
     'L0_gnn_W1': 2.668,
     'L0_gnn_b1': 30.149,
     'L0_gnn_b2': 8.0,
     'L0_gnn_b_hh': 3.438,
     'L2_gnn_b_msg': 8.0}
    for name, (base, spread) in spreads.items():
        noise = np.random.default_rng([zlib.crc32(name.encode()), seed]).standard_normal(out[name].shape)
        drawn = base * np.exp(spread * noise) if base else spread * noise
        out[name] = jnp.asarray(drawn.astype(out[name].dtype))
    for name, factor in factors.items():
        out[name] = (out[name] * factor).astype(out[name].dtype)
    return out
```

```python
from contextlib import ExitStack

import concourse.bass as bass
from concourse import mybir

F32 = mybir.dt.float32
BF16 = mybir.dt.bfloat16
I32 = mybir.dt.int32
ALU = mybir.AluOpType
ACT = mybir.ActivationFunctionType
AX_X = mybir.AxisListType.X

P = 128
N, D, E = 100000, 64, 25000
NODES = 1024
NG = NODES // P
TILES = 2
EG = 2 * TILES
G = NG + EG
PAIRS = -(-N // NODES)
ROWS = PAIRS * NODES
assert PAIRS * TILES * P >= E and ROWS - N > P
W = G * D
RAW = 2 * W
CH = 4
EPS = 1e-5
RSQRT_SEED = float(0x5F3759DF)
PHASES = 5
CHUNKS = {1: 3, 2: 3, 3: 3, 4: 2}
LAST_ROWS = N - (PAIRS - 1) * NODES
LAST_P = LAST_ROWS // NG
assert LAST_P * NG == LAST_ROWS
NEWTON = 12
STORE_SKEW = {1: 3, 2: 3, 3: 3, 4: 2}
WEIGHT_DMAS = 45


class Pair:

    def __init__(self, c, reg=None):
        self.c, self.reg = c, reg
        self.p = c % 2

    def __sub__(self, k):
        return Pair(self.c - k, self.reg)

    def times(self, m, add):
        n = m * self.c + add
        return n if self.reg is None else self.reg * (2 * m) + n

    def half(self, m, add):
        n = m * (self.c // 2) + add
        return n if self.reg is None else self.reg * m + n

    @property
    def real(self):
        return self.reg is not None or 0 <= self.c < PAIRS

    @property
    def index(self):
        return self.c if self.reg is None else self.reg * 2 + self.c


def steps(eng, body, skew):
    total = PAIRS + skew
    lead = skew + 2 + skew % 2
    tail = skew + 1 + (total - lead - skew - 1) % 2
    for s in range(lead):
        body(Pair(s))
    with eng.Fori(0, (total - lead - tail) // 2) as i:
        body(Pair(lead, i))
        body(Pair(lead + 1, i))
    for s in range(total - tail, total):
        body(Pair(s))


class Event:

    def __init__(self, sem, per):
        self.sem, self.per = sem, per

    def end(self, ph):
        return sum(PAIRS * n for q, n in self.per.items() if q < ph)

    def at(self, ph, b, k=0):
        return b.times(self.per[ph], self.end(ph) + k + 1)


class Landed:

    def __init__(self, sems, per):
        self.sems, self.per = sems, per

    def sem(self, b):
        return self.sems[b.p]

    def end(self, ph):
        return sum(16 * n * (PAIRS // 2) for q, n in self.per.items() if q < ph)

    def at(self, ph, b):
        n = 16 * self.per[ph]
        return b.half(n, self.end(ph) + n)


def build(nc, x_in, gather_rows, key_cols, key_rows, attr_rows, attr64, weights, out):
    w = weights
    dram = lambda name, shape, dt: nc.dram_tensor(name, shape, dt, kind="Internal").ap()
    x_dram = dram("x_nodes", [ROWS, D], F32)
    ends_dram = dram("x_edge_ends", [PAIRS, P, EG * D], F32)
    rows_dram = dram("scatter_rows", [PAIRS, P, 2 * EG], I32)
    table = [dram("sums0", [ROWS, D], F32), dram("sums1", [ROWS, 2 * D], F32),
             dram("sums2", [ROWS, D + 1], F32), dram("sums3", [ROWS, D], F32)]
    width = [D, 2 * D, D + 1, D]
    halves1 = table[1].rearrange("n (h d) -> (n h) d", h=2)

    def nodes_of(t):
        return t.rearrange("(b p r) d -> b p (r d)", p=P, r=NG)

    with ExitStack() as ctx:
        def sb(name, shape, dt=F32):
            return ctx.enter_context(nc.sbuf_tensor(name, shape, dt))

        def ps(name, shape):
            return ctx.enter_context(nc.psum_tensor(name, shape, F32))

        def sem(name):
            return ctx.enter_context(nc.semaphore(name))

        def event(name, per):
            return Event(sem(name), per)

        def landed(name, per):
            return Landed([sem(name + "_0"), sem(name + "_1")], per)

        ident = sb("ident", [P, P])
        before = sb("before", [P, P])
        spare = sb("spare", [P, EG])
        spare_i = sb("spare_i", [P, EG], I32)
        zeros = sb("zeros", [P, 2 * NG * D])
        w_gru = sb("w_gru", [P, 4 * D])
        w_h = sb("w_h", [P, 2 * D])
        w_e = sb("w_e", [1, 2 * D])
        b_h = sb("b_h", [P, 1])
        w_m0 = sb("w_m0", [P, D])
        w_self = sb("w_self", [P, 2 * D])
        w_nb = sb("w_nb", [P, 2 * D])
        w_m2 = sb("w_m2", [P, D])
        w_u2 = sb("w_u2", [P, D])
        w_m3 = sb("w_m3", [P, D])
        w_u3 = sb("w_u3", [P, 2 * D])
        eps1 = sb("eps1", [P, 1])
        eps1p = sb("eps1p", [P, 1])
        BIAS = {"gru": (0, 512), "m0": (512, 128), "self": (640, 256), "nb": (896, 256), "m2": (1152, 128),
                "u2": (1280, 256), "m3": (1536, 128), "u3": (1664, 256)}
        NB = 1920
        bias = sb("bias", [65, NB])
        bias_hh = sb("bias_hh", [65, 512])
        bias_hi = sb("bias_hi", [65, NB], BF16)
        bias_mid = sb("bias_mid", [65, NB], BF16)
        bias_lo = sb("bias_lo", [65, NB], BF16)
        bias_r1 = sb("bias_r1", [65, NB])
        bias_r2 = sb("bias_r2", [65, NB])
        bias3 = sb("bias3", [65, NB], BF16)
        ones65 = sb("ones65", [65, P], BF16)

        two = range(2)
        rows = [sb(f"rows{p}", [P, 4 * W]) for p in two]
        g_rows = [sb(f"g_rows{p}", [P, EG], I32) for p in two]
        s_rows = [sb(f"s_rows{p}", [P, 2 * EG], I32) for p in two]
        keyc = [sb(f"keyc{p}", [P, EG], I32) for p in two]
        keyr = [sb(f"keyr{p}", [P, EG * P], I32) for p in two]
        attr_r = [sb(f"attr_r{p}", [1, TILES * P]) for p in two]
        xt = [sb(f"xt{p}", [P, CH * P]) for p in two]
        gates = [sb(f"gates{p}", [P, G * 2 * D]) for p in two]
        pre_n = [sb(f"pre_n{p}", [P, W]) for p in two]
        act_n = [sb(f"act_n{p}", [P, W]) for p in two]
        diff = [sb(f"diff{p}", [P, W]) for p in two]
        y = [sb(f"y{p}", [P, W]) for p in two]
        sq = [sb(f"sq{p}", [P, W]) for p in two]
        xn = [sb(f"xn{p}", [P, W]) for p in two]
        same = [sb(f"same{p}", [P, EG, P]) for p in two]
        earlier = sb("earlier", [P, EG, P])
        et = [sb(f"et{p}", [P, TILES * P]) for p in two]
        hid = [sb(f"hid{p}", [P, TILES * P]) for p in two]
        msg = [sb(f"msg{p}", [P, 4 * D + 2]) for p in two]
        summed = [sb(f"summed{p}", [P, EG * (D + 1)]) for p in two]
        tot = sb("tot", [P, G])
        ssq = sb("ssq", [P, G])
        var = sb("var", [P, G])
        seed = sb("seed", [P, G], I32)
        rinv_i = sb("rinv_i", [P, G], I32)
        nt_a = sb("nt_a", [P, G])
        nt_b = sb("nt_b", [P, G])
        cnt = sb("cnt", [P, G])
        rcnt = sb("rcnt", [P, G])
        key_f = sb("key_f", [P, EG])
        dup = sb("dup", [P, EG])
        dup1 = sb("dup1", [P, EG])
        off = sb("off", [P, EG])
        off1 = sb("off1", [P, EG])
        row_f = sb("row_f", [P, EG])

        pT = ps("pT", [P, 2, 512])
        pG = ps("pG", [P, 4, 512])
        pEM = ps("pEM", [P, 512])
        pE, pM = pEM[:, 0:256], pEM[:, 256:512]
        pD = ps("pD", [P, 512])

        w_landed = sem("w_landed")
        zero0 = sem("zero0")
        zeroed = landed("zeroed", {0: 1, 1: 1, 2: 1})
        in_rows = landed("in_rows", {1: 3, 2: 3, 3: 3, 4: 2})
        in_gidx = landed("in_gidx", {0: 1, 1: 1, 2: 1, 3: 1})
        in_keys = landed("in_keys", {0: 3, 1: 2, 2: 2, 3: 2})
        in_sidx = landed("in_sidx", {1: 1, 2: 1, 3: 1})
        in_attr = landed("in_attr", {3: 1})
        gathered = landed("gathered", {0: 4, 1: 4, 2: 4, 3: 2})
        st_x = landed("st_x", {1: 1, 2: 1, 3: 1, 4: 1})
        st_ends = landed("st_ends", {0: 1, 1: 1, 2: 1})
        st_rows = landed("st_rows", {0: 1})
        dst_added = sem("dst_added")
        src_added = sem("src_added")

        ready = sem("ready")
        pool_ready = sem("pool_ready")
        held = [sem("held_sp"), sem("held_pool")]
        prep_w = sem("prep_w")
        e03 = {0: 1, 1: 1, 2: 1, 3: 1}
        u14 = {1: 1, 2: 1, 3: 1, 4: 1}
        t_done = event("t_done", CHUNKS)
        t_copied = event("t_copied", CHUNKS)
        g_done = event("g_done", CHUNKS)
        g_used = event("g_used", {1: 3, 2: 3, 4: 2})
        gate_done = event("gate_done", {1: 3})
        rn_done = event("rn_done", {1: 3})
        tanh_done = event("tanh_done", {1: 1})
        diff_done = event("diff_done", {1: 1})
        zd_done = event("zd_done", {1: 1})
        cnt_done = event("cnt_done", {3: 2})
        pre_done = event("pre_done", {3: 1, 4: 1})
        gelu_done = event("gelu_done", {4: 2})
        y_done = event("y_done", {1: 1, 2: 1, 3: 3, 4: 1})
        sum_done = event("sum_done", u14)
        cen_done = event("cen_done", u14)
        sq_done = event("sq_done", u14)
        ssq_done = event("ssq_done", u14)
        newton = event("newton", {q: NEWTON for q in u14})
        ln_done = event("ln_done", u14)
        e_trans = event("e_trans", e03)
        e_copied = event("e_copied", e03)
        h_mm = event("h_mm", {0: 1})
        h_act = event("h_act", {0: 1})
        m_mm = event("m_mm", e03)
        m_act = event("m_act", e03)
        s_built = event("s_built", e03)
        prep = event("prep", {0: 10})
        d_mm = event("d_mm", e03)
        d_act = event("d_act", e03)

        def hold(eng):
            eng.sem_inc(held[eng is nc.gpsimd], 1)

        def dst_at(ph, b, t):
            return b.times(32, 32 * PAIRS * ph + 16 * (t + 1))

        def src_at(b, t):
            return b.times(32, 16 * (t + 1))

        def bias_of(name, n=None):
            a, m = BIAS[name]
            return bias3[:, a:a + (n or m)]

        def buf(ph, b, k):
            return (CHUNKS[ph] * b.p + k) % 2

        def groups(t, a, n, c=D):
            return t[:, a * c:(a + n) * c].rearrange("p (g c) -> p g c", c=c)

        def spread(t, n, c=D):
            return t[:, 0:n].unsqueeze(2).broadcast_to([P, n, c])

        def x_of(ph, b, a, n):
            if ph in (1, 3):
                return groups(rows[b.p], a, n, 2 * D)[:, :, 0:D]
            return groups(rows[b.p], a, n)

        def sums_of(ph, b, a, n):
            if ph == 1:
                return groups(rows[b.p], a, n, 2 * D)[:, :, D:2 * D]
            return groups(rows[b.p][:, RAW:4 * W], a, n, width[ph - 1])

        updated = {1: G, 2: G, 3: NG + TILES, 4: NG}

        block = ctx.enter_context(nc.Block())

        @block.sync
        def _(sp):
            def put(dst, src):
                sp.dma_start(dst, src).then_inc(w_landed, 16)
                return 16

            sp.wait_ge(ready, 2)
            put(w_gru[0:D, 0:2 * D], w["L0_W_hh"][:, 0:2 * D])
            put(w_gru[0:D, 3 * D:4 * D], w["L0_W_hh"][:, 2 * D:3 * D])
            put(w_gru[D:P, 0:3 * D], w["L0_W_ih"])
            put(w_h[:, :], w["L0_W1"][0:P, :])
            put(w_e[:, :], w["L0_W1"][P:P + 1, :])
            put(b_h[:, :], w["L0_b1"].rearrange("(p o) -> p o", o=1))
            put(w_m0[:, :], w["L0_W2"])
            for dst, name in ((w_self, "L1_w0_w"), (w_nb, "L1_w1_w"), (w_u3, "L3_W_upd")):
                put(dst[0:D, 0:D], w[name])
                put(dst[D:P, D:P], w[name])
            put(w_m2[:, :], w["L2_W_msg"])
            put(w_u2[:, :], w["L2_W_upd"])
            put(w_m3[:, :], w["L3_W_msg"])
            put(eps1[:, :], w["L3_eps"].unsqueeze(0).broadcast_to([P, 1]))
            for rep in range(2):
                put(bias[:, rep * 256:rep * 256 + 3 * D], w["L0_b_ih"].unsqueeze(0).broadcast_to([65, 3 * D]))
                put(bias_hh[:, rep * 256:rep * 256 + 2 * D], w["L0_b_hh"][0:2 * D].unsqueeze(0).broadcast_to([65, 2 * D]))
                put(bias_hh[:, rep * 256 + 3 * D:rep * 256 + 4 * D],
                    w["L0_b_hh"][2 * D:3 * D].unsqueeze(0).broadcast_to([65, D]))
            for name, src in (("m0", "L0_b2"), ("self", "L1_w0_b"), ("nb", "L1_w1_b"), ("m2", "L2_b_msg"),
                              ("u2", "L2_b_upd"), ("m3", "L3_b_msg"), ("u3", "L3_b_upd")):
                a, m = BIAS[name]
                for c in range(a, a + m, D):
                    put(bias[:, c:c + D], w[src].unsqueeze(0).broadcast_to([65, D]))

            def load_gidx(ph, b):
                if (b - 2).real:
                    sp.wait_ge(gathered.sem(b), gathered.at(ph, b - 2))
                hold(sp)
                sp.dma_start(g_rows[b.p][:, :], gather_rows[b.index]).then_inc(in_gidx.sem(b), 16)

            def load_keys(ph, b):
                if (b - 2).real:
                    sp.wait_ge(s_built.sem, s_built.at(ph, b - 2))
                    if ph == 0:
                        hold(sp)
                        sp.wait_ge(prep.sem, prep.at(0, b - 2, 0))
                        hold(sp)
                        sp.wait_ge(h_mm.sem, h_mm.at(0, b - 2))
                hold(sp)
                first = 0 if ph < 2 else TILES
                sp.dma_start(keyr[b.p][:, first * P:EG * P],
                             key_rows[b.index][first * P:EG * P].unsqueeze(0).broadcast_to([P, (EG - first) * P])
                             ).then_inc(in_keys.sem(b), 16)
                sp.dma_start(keyc[b.p][:, :], key_cols[b.index]).then_inc(in_keys.sem(b), 16)
                if ph == 0:
                    sp.dma_start(attr_r[b.p][:, :], attr_rows[b.index].unsqueeze(0)).then_inc(in_keys.sem(b), 16)

            def zero(ph, b):
                n = NG * width[ph + 1]
                sp.dma_start(nodes_of(table[ph + 1])[b.index], zeros[:, 0:n]).then_inc(zeroed.sem(b), 16)

            def load_rows(ph, b, last=False):
                if (b - 2).real:
                    sp.wait_ge(y_done.sem, y_done.at(ph, b - 2, y_done.per[ph] - 1))
                hold(sp)
                if ph > 1:
                    x, to = x_dram, x_of(ph, b, 0, NG)
                    src = x[:, :].rearrange("(b p r) d -> b p r d", p=P, r=NG)[b.index]
                elif last:
                    to = x_of(1, b, 0, NG)[0:LAST_P]
                    src = x_in[(PAIRS - 1) * NODES:N, :].rearrange("(p r) d -> p r d", r=NG)
                else:
                    to = x_of(1, b, 0, NG)
                    src = x_in[0:(PAIRS - 1) * NODES, :].rearrange("(b p r) d -> b p r d", p=P, r=NG)[b.index]
                sp.dma_start(to, src).then_inc(in_rows.sem(b), 16)
                sp.dma_start(sums_of(ph, b, 0, NG),
                             table[ph - 1].rearrange("(b p r) d -> b p r d", p=P, r=NG)[b.index]
                             ).then_inc(in_rows.sem(b), 16)
                if ph < 4:
                    m = updated[ph] - NG
                    ends = ends_dram[b.index].rearrange("p (g c) -> p g c", c=D)
                    sp.dma_start(x_of(ph, b, NG, m), ends if ph < 3 else ends[:, 0:EG:2, :]
                                 ).then_inc(in_rows.sem(b), 16)

            def load_sidx(ph, b):
                if (b - 2).real:
                    sp.wait_ge(dst_added, dst_at(ph, b - 2, 1))
                    if ph == 1:
                        hold(sp)
                        sp.wait_ge(src_added, src_at(b - 2, 1))
                hold(sp)
                sp.dma_start(s_rows[b.p][:, :], rows_dram[b.index]).then_inc(in_sidx.sem(b), 16)

            def load_attr(b):
                if (b - 2).real:
                    sp.wait_ge(e_trans.sem, e_trans.at(3, b - 2))
                hold(sp)
                sp.dma_start(groups(xn[b.p], NG, EG)[:, 1:EG:2, :],
                             attr64[:, b.index, :].rearrange("p (t c) -> p t c", c=D)).then_inc(in_attr.sem(b), 16)

            def store(ph, b, last=False):
                sp.wait_ge(ln_done.sem, ln_done.at(ph, b))
                hold(sp)
                v = xn[b.p]
                if ph < 4:
                    sp.dma_start(nodes_of(x_dram)[b.index], v[:, 0:NG * D]).then_inc(st_x.sem(b), 16)
                elif last:
                    sp.dma_start(out[(PAIRS - 1) * NODES:N, :].rearrange("(p r) d -> p (r d)", r=NG),
                                 v[0:LAST_P, 0:NG * D]).then_inc(st_x.sem(b), 16)
                else:
                    sp.dma_start(nodes_of(out[0:(PAIRS - 1) * NODES, :])[b.index], v[:, 0:NG * D]
                                 ).then_inc(st_x.sem(b), 16)
                if ph < 3:
                    sp.dma_start(ends_dram[b.index], v[:, NG * D:G * D]).then_inc(st_ends.sem(b), 16)

            def body0(s):
                if s.real:
                    load_gidx(0, s)
                    load_keys(0, s)
                    zero(0, s)
                b = s - 1
                if b.real:
                    sp.wait_ge(gathered.sem(b), gathered.at(0, b))
                    hold(sp)
                    sp.dma_start(ends_dram[b.index], rows[b.p][:, NG * D:G * D]).then_inc(st_ends.sem(b), 16)
                b = s - 2
                if b.real:
                    sp.wait_ge(prep.sem, prep.at(0, b, 9))
                    hold(sp)
                    sp.dma_start(rows_dram[b.index], s_rows[b.p][:, :]).then_inc(st_rows.sem(b), 16)

            steps(sp, body0, 2)

            for ph in range(1, PHASES):
                sp.wait_ge(dst_added, 32 * PAIRS * ph)
                if ph == 2:
                    sp.wait_ge(src_added, 32 * PAIRS)
                for q in two:
                    sp.wait_ge(st_ends.sems[q], st_ends.end(ph))
                    if ph == 1:
                        sp.wait_ge(st_rows.sems[q], st_rows.end(ph))
                    if ph > 1:
                        sp.wait_ge(st_x.sems[q], st_x.end(ph))
                    if ph < 4:
                        sp.wait_ge(zeroed.sems[q], zeroed.end(ph))

                def body(s, ph=ph):
                    last = s.reg is None and s.c == PAIRS - 1
                    if s.real:
                        load_rows(ph, s, last)
                        if ph < 4:
                            load_gidx(ph, s)
                    if ph < 4 and (s - 1).real:
                        load_keys(ph, s - 1)
                    if ph == 3 and (s - 2).real:
                        load_attr(s - 2)
                    if ph < 4 and (s - 3).real:
                        load_sidx(ph, s - 3)
                    b = s - STORE_SKEW[ph]
                    if b.real:
                        store(ph, b, b.reg is None and b.c == PAIRS - 1)
                        if ph < 3:
                            zero(ph, b)

                steps(sp, body, 3)
            for q in two:
                sp.wait_ge(st_x.sems[q], st_x.end(PHASES))

        @block.gpsimd
        def _(pool):
            pool.memset(ident[:, :], 0.0).then_inc(pool_ready, 1)
            pool.memset(before[:, :], 1.0).then_inc(pool_ready, 1)
            pool.wait_ge(pool_ready, 2)
            pool.affine_select(out=ident[:, :], in_=ident[:, :], compare_op=ALU.not_equal, fill=1.0, base=0,
                               pattern=[[-1, P]], channel_multiplier=1).then_inc(pool_ready, 1)
            pool.affine_select(out=before[:, :], in_=before[:, :], compare_op=ALU.is_gt, fill=0.0, base=0,
                               pattern=[[-1, P]], channel_multiplier=1).then_inc(pool_ready, 1)
            pool.iota(spare_i[:, :], pattern=[[0, EG]], base=N + 1, channel_multiplier=1).then_inc(pool_ready, 1)

            def gather(ph, b, j):
                src = x_in if ph == 0 else table[ph - 1]
                to = x_of(0, b, NG + j, 1) if ph == 0 else sums_of(ph, b, NG + j, 1)
                col = j if ph == 3 else (j % 2) * TILES + j // 2
                pool.indirect_dma_start(to[:, 0, :], None, src,
                                        bass.IndirectOffsetOnAxis(g_rows[b.p][:, col:col + 1], 0)
                                        ).then_inc(gathered.sem(b), 16)

            def may_gather(ph, b):
                pool.wait_ge(in_gidx.sem(b), in_gidx.at(ph, b))
                if not (b - 2).real:
                    return
                if ph == 0:
                    pool.wait_ge(e_trans.sem, e_trans.at(0, b - 2))
                    pool.wait_ge(st_ends.sem(b), st_ends.at(0, b - 2))
                elif ph == 1:
                    pool.wait_ge(t_done.sem, t_done.at(1, b - 2, 2))
                elif ph == 2:
                    pool.wait_ge(y_done.sem, y_done.at(2, b - 2))
                else:
                    pool.wait_ge(pre_done.sem, pre_done.at(3, b - 2))

            def scatter(ph, b, t):
                if t == 0:
                    pool.wait_ge(d_act.sem, d_act.at(ph, b))
                    if ph:
                        pool.wait_ge(in_sidx.sem(b), in_sidx.at(ph, b))
                    else:
                        pool.wait_ge(prep.sem, prep.at(0, b, 9))
                first = b.reg is None and b.c == 0 and t == 0
                if not first:
                    pool.wait_ge(dst_added, dst_at(ph, b, t - 1))
                n = D + 1 if ph == 2 else D
                dst = halves1 if ph == 1 else table[ph]
                hold(pool)
                col = TILES + t + (EG if ph == 1 else 0)
                at = (TILES + t) * D if ph == 1 else t * n
                pool.indirect_dma_start(dst, bass.IndirectOffsetOnAxis(s_rows[b.p][:, col:col + 1], 0),
                                        summed[b.p][:, at:at + n], None, compute_op=ALU.add).then_inc(dst_added, 16)
                if ph == 1:
                    if not first:
                        pool.wait_ge(src_added, src_at(b, t - 1))
                    hold(pool)
                    col = t + EG
                    pool.indirect_dma_start(dst, bass.IndirectOffsetOnAxis(s_rows[b.p][:, col:col + 1], 0),
                                            summed[b.p][:, t * D:(t + 1) * D], None, compute_op=ALU.add
                                            ).then_inc(src_added, 16)

            for ph in range(4):
                if ph == 0:
                    pool.wait_ge(zero0, 16)
                else:
                    for q in two:
                        pool.wait_ge(zeroed.sems[q], zeroed.end(ph))
                    pool.wait_ge(dst_added, 32 * PAIRS * ph)
                    if ph == 2:
                        pool.wait_ge(src_added, 32 * PAIRS)
                skew = 2 if ph == 0 else 4

                def body(s, ph=ph, skew=skew):
                    b = s - skew
                    m = TILES if ph == 3 else EG
                    if s.real:
                        may_gather(ph, s)
                    for t in range(TILES):
                        if b.real:
                            scatter(ph, b, t)
                        if s.real:
                            for j in range(t * m // 2, (t + 1) * m // 2):
                                gather(ph, s, j)

                steps(pool, body, skew)
            pool.wait_ge(dst_added, 32 * PAIRS * 4)

        @block.tensor
        def _(pe):
            pe.wait_ge(pool_ready, 5)
            pe.wait_ge(ready, 3)

            def transpose_chunk(ph, b, k):
                last = min(updated[ph], (k + 1) * CH)
                if k == 0:
                    pe.wait_ge(in_rows.sem(b), in_rows.at(ph, b))
                    if ph > 2:
                        pe.wait_ge(pre_done.sem, pre_done.at(ph, b))
                if k == 2 and ph == 1:
                    pe.wait_ge(gathered.sem(b), gathered.at(ph, b))
                c = buf(ph, b, k)
                if b.reg is not None or CHUNKS[ph] * b.c + k >= 2:
                    pe.wait_ge(t_copied.sem, t_copied.at(ph, b, k - 2))
                per = 1 if ph in (1, 3) else 2
                a = W if ph == 4 else 0
                for i, g in enumerate(range(k * CH, last, per)):
                    at = a + g * P // per
                    t = pe.transpose(pT[:, c, i * P:(i + 1) * P], rows[b.p][:, at:at + P], ident[:, :])
                t.then_inc(t_done.sem, 1)

            def update_chunk(ph, b, k):
                pe.wait_ge(t_copied.sem, t_copied.at(ph, b, k))
                c = buf(ph, b, k)
                if b.reg is not None or CHUNKS[ph] * b.c + k >= 2:
                    used = y_done if ph == 3 else g_used
                    pe.wait_ge(used.sem, used.at(ph, b, k - 2))
                n = min(updated[ph], (k + 1) * CH) - k * CH
                x = xt[c]
                if ph == 1:
                    for g in range(n):
                        o = pG[:, 2 * c + g // 2, (g % 2) * 256:(g % 2 + 1) * 256]
                        if g % 2 == 0:
                            pe.matmul(pG[:, 2 * c + g // 2, :], ones65[:, :], bias_of("gru"), start=True, stop=False)
                        m = pe.matmul(o, x[:, g * P:(g + 1) * P], w_gru[:, :], start=False, stop=(g % 2 == 1))
                else:
                    name = {2: "self", 3: "u2", 4: "u3"}[ph]
                    wt = {2: w_self, 3: w_u2, 4: w_u3}[ph]
                    per = D if ph == 3 else 2 * D
                    pe.matmul(pG[:, c, 0:n * D], ones65[:, :], bias_of(name, n * D), start=True, stop=False)
                    for i in range(n * D // per):
                        m = pe.matmul(pG[:, c, i * per:(i + 1) * per], x[:, i * P:(i + 1) * P], wt[:, :],
                                      start=False, stop=(i == n * D // per - 1))
                m.then_inc(g_done.sem, 1)

            def edge_transpose(ph, b):
                if ph == 0:
                    pe.wait_ge(gathered.sem(b), gathered.at(0, b))
                    src = rows[b.p]
                else:
                    pe.wait_ge(ln_done.sem, ln_done.at(ph, b))
                    src = xn[b.p]
                if ph == 3:
                    pe.wait_ge(in_attr.sem(b), in_attr.at(3, b))
                if (b - 1).real:
                    last = h_act if ph == 0 else m_act
                    pe.wait_ge(last.sem, last.at(ph, b - 1))
                for t in range(TILES):
                    m = pe.transpose(pE[:, t * P:(t + 1) * P], src[:, (NG + 2 * t) * D:(NG + 2 * t + 2) * D], ident[:, :])
                m.then_inc(e_trans.sem, 1)

            def hidden(b):
                pe.wait_ge(e_copied.sem, e_copied.at(0, b))
                pe.wait_ge(in_keys.sem(b), in_keys.at(0, b))
                pe.matmul(pM[:, 0:TILES * P], w_h[:, :], et[b.p][:, :], start=True, stop=False)
                pe.matmul(pM[:, 0:TILES * P], w_e[:, :], attr_r[b.p][:, :], start=False, stop=True).then_inc(h_mm.sem, 1)

            def messages(ph, b):
                if ph == 0:
                    pe.wait_ge(h_act.sem, h_act.at(0, b))
                else:
                    pe.wait_ge(e_copied.sem, e_copied.at(ph, b))
                if (b - 1).real:
                    pe.wait_ge(m_act.sem, m_act.at(ph, b - 1))
                src, wt, name = [(hid, w_m0, "m0"), (et, w_nb, "nb"), (et, w_m2, "m2"), (et, w_m3, "m3")][ph]
                o = pG[:, 0, :] if ph == 0 else pM
                n = 2 * D if ph == 1 else D
                pe.matmul(o[:, 0:TILES * n], ones65[:, :], bias_of(name), start=True, stop=False)
                for t in range(TILES):
                    m = pe.matmul(o[:, t * n:(t + 1) * n], src[b.p][:, t * P:(t + 1) * P], wt[:, :],
                                  start=False, stop=(t == TILES - 1))
                m.then_inc(m_mm.sem, 1)

            def sum_by_key(ph, b):
                pe.wait_ge(m_act.sem, m_act.at(ph, b))
                pe.wait_ge(s_built.sem, s_built.at(ph, b))
                if (b - 1).real:
                    pe.wait_ge(d_act.sem, d_act.at(ph, b - 1))
                v = msg[b.p]
                if ph == 1:
                    for j in range(EG):
                        a = (j % TILES) * 2 * D + (D if j < TILES else 0)
                        m = pe.matmul(pD[:, j * D:(j + 1) * D], same[b.p][:, j, :], v[:, a:a + D], start=True, stop=True)
                else:
                    n = D + 1 if ph == 2 else D
                    for t in range(TILES):
                        m = pe.matmul(pD[:, t * n:(t + 1) * n], same[b.p][:, TILES + t, :], v[:, t * n:(t + 1) * n],
                                      start=True, stop=True)
                m.then_inc(d_mm.sem, 1)

            def body0(s):
                edge_transpose(0, s)
                hidden(s)
                messages(0, s)
                sum_by_key(0, s)

            steps(pe, body0, 0)

            for ph in range(1, 4):
                def body(s, ph=ph):
                    if s.real:
                        transpose_chunk(ph, s, 0)
                        transpose_chunk(ph, s, 1)
                    if (s - 3).real:
                        sum_by_key(ph, s - 3)
                    if s.real:
                        update_chunk(ph, s, 0)
                        transpose_chunk(ph, s, 2)
                        update_chunk(ph, s, 1)
                    if (s - 2).real:
                        edge_transpose(ph, s - 2)
                    if s.real:
                        update_chunk(ph, s, 2)
                    if (s - 2).real:
                        messages(ph, s - 2)

                steps(pe, body, 3)

            def body4(s):
                transpose_chunk(4, s, 0)
                transpose_chunk(4, s, 1)
                update_chunk(4, s, 0)
                update_chunk(4, s, 1)

            steps(pe, body4, 0)

        @block.scalar
        def _(act):
            act.wait_ge(ready, 1)
            n = PAIRS // 2
            act.dma_start(table[0].rearrange("(p k r) d -> p k (r d)", p=P, k=n),
                          zeros[:, :].unsqueeze(1).broadcast_to([P, n, 2 * NG * D])
                          ).then_inc(zero0, 16)
            act.wait_ge(ready, 3)

            def copy_chunk(ph, b, k):
                act.wait_ge(t_done.sem, t_done.at(ph, b, k))
                c = buf(ph, b, k)
                if b.reg is not None or CHUNKS[ph] * b.c + k >= 2:
                    act.wait_ge(g_done.sem, g_done.at(ph, b, k - 2))
                n = min(updated[ph], (k + 1) * CH) - k * CH
                n = n * P if ph in (1, 3) else n * D
                act.copy(xt[c][:, 0:n], pT[:, c, 0:n]).then_inc(t_copied.sem, 1)

            def gate_chunk(b, k):
                act.wait_ge(g_done.sem, g_done.at(1, b, k))
                if (b - 2).real:
                    act.wait_ge(zd_done.sem, zd_done.at(1, b - 2))
                c = buf(1, b, k)
                act.activation(groups(gates[b.p], k * CH, CH, 2 * D),
                               pG[:, 2 * c:2 * c + 2, :].rearrange("p a (g c) -> p (a g) c", c=256)[:, :, 0:2 * D],
                               ACT.Sigmoid).then_inc(gate_done.sem, 1)

            def square(ph, b):
                act.wait_ge(cen_done.sem, cen_done.at(ph, b))
                if (b - 2).real:
                    act.wait_ge(ssq_done.sem, ssq_done.at(ph, b - 2))
                n = updated[ph] * D
                act.activation(sq[b.p][:, 0:n], y[b.p][:, 0:n], ACT.Square).then_inc(sq_done.sem, 1)

            def copy_edges(ph, b):
                act.wait_ge(e_trans.sem, e_trans.at(ph, b))
                if (b - 2).real:
                    free = h_mm if ph == 0 else m_mm
                    act.wait_ge(free.sem, free.at(ph, b - 2))
                act.copy(et[b.p][:, :], pE[:, 0:TILES * P]).then_inc(e_copied.sem, 1)

            def act_messages(ph, b):
                act.wait_ge(m_mm.sem, m_mm.at(ph, b))
                if (b - 2).real:
                    act.wait_ge(d_mm.sem, d_mm.at(ph, b - 2))
                if ph == 2:
                    i = act.activation(groups(msg[b.p], 0, TILES, D + 1)[:, :, 0:D], groups(pM, 0, TILES), ACT.Relu)
                elif ph == 3:
                    i = act.activation(msg[b.p][:, 0:TILES * D], pM[:, 0:TILES * D], ACT.Gelu_apprx_tanh)
                elif ph == 1:
                    i = act.copy(msg[b.p][:, 0:TILES * 2 * D], pM[:, 0:TILES * 2 * D])
                else:
                    i = act.copy(msg[b.p][:, 0:TILES * D], pG[:, 0, 0:TILES * D])
                i.then_inc(m_act.sem, 1)

            def copy_sums(ph, b):
                act.wait_ge(d_mm.sem, d_mm.at(ph, b))
                if (b - 2).real:
                    act.wait_ge(dst_added, dst_at(ph, b - 2, 1))
                    if ph == 1:
                        act.wait_ge(src_added, src_at(b - 2, 1))
                n = {0: TILES * D, 1: EG * D, 2: TILES * (D + 1), 3: TILES * D}[ph]
                act.copy(summed[b.p][:, 0:n], pD[:, 0:n]).then_inc(d_act.sem, 1)

            def body0(b):
                copy_edges(0, b)
                act.wait_ge(h_mm.sem, h_mm.at(0, b))
                if (b - 2).real:
                    act.wait_ge(m_mm.sem, m_mm.at(0, b - 2))
                act.activation(hid[b.p][:, :], pM[:, 0:TILES * P], ACT.Relu, bias=b_h[:, 0:1]).then_inc(h_act.sem, 1)
                act_messages(0, b)
                copy_sums(0, b)

            steps(act, body0, 0)

            for ph in range(1, 4):
                if ph == 2:
                    for q in two:
                        last = act.activation(groups(msg[q], 0, TILES, D + 1)[:, :, D:D + 1],
                                              groups(zeros, 0, TILES, D)[:, :, 0:1], ACT.Copy, bias=1.0)
                def body(s, ph=ph):
                    if s.real:
                        copy_chunk(ph, s, 0)
                        copy_chunk(ph, s, 1)
                    if (s - 3).real:
                        copy_sums(ph, s - 3)
                    if s.real:
                        if ph == 1:
                            gate_chunk(s, 0)
                        copy_chunk(ph, s, 2)
                        if ph == 1:
                            gate_chunk(s, 1)
                    if (s - 1).real:
                        square(ph, s - 1)
                    if (s - 2).real:
                        copy_edges(ph, s - 2)
                    if s.real and ph == 1:
                        gate_chunk(s, 2)
                        act.wait_ge(g_used.sem, g_used.at(1, s, 2))
                        if (s - 2).real:
                            act.wait_ge(diff_done.sem, diff_done.at(1, s - 2))
                        act.activation(act_n[s.p][:, :], pre_n[s.p][:, :], ACT.Tanh).then_inc(tanh_done.sem, 1)
                    if (s - 2).real:
                        act_messages(ph, s - 2)

                steps(act, body, 3)

            def body4(s):
                if s.real:
                    copy_chunk(4, s, 0)
                    copy_chunk(4, s, 1)
                if (s - 1).real:
                    square(4, s - 1)
                if s.real:
                    for k in range(2):
                        act.wait_ge(g_done.sem, g_done.at(4, s, k))
                        if (s - 2).real:
                            act.wait_ge(y_done.sem, y_done.at(4, s - 2))
                        act.activation(act_n[s.p][:, k * CH * D:(k + 1) * CH * D], pG[:, buf(4, s, k), 0:CH * D],
                                       ACT.Gelu_apprx_tanh).then_inc(g_used.sem, 1)

            steps(act, body4, 1)

        @block.vector
        def _(dve):
            dve.memset(zeros[:, :], 0.0).then_inc(ready, 1)
            for t in (w_gru, w_self, w_nb, w_u3, bias, bias_hh, bias3):
                dve.memset(t[:, :], 0.0)
            dve.memset(ones65[:, :], 1.0).then_inc(ready, 1)
            dve.wait_ge(pool_ready, 5)
            dve.tensor_copy(spare[:, :], spare_i[:, :])
            dve.wait_ge(w_landed, 16 * WEIGHT_DMAS)
            dve.tensor_tensor(w_self[:, :], w_self[:, :], ident[:, :], ALU.add).then_inc(prep_w, 1)
            dve.tensor_scalar(w_gru[:, D:2 * D], w_gru[:, D:2 * D], -1.0, None, ALU.mult).then_inc(prep_w, 1)
            dve.tensor_scalar(eps1p[:, :], eps1[:, :], 1.0, None, ALU.add).then_inc(prep_w, 1)
            dve.tensor_tensor(bias[:, 0:512], bias[:, 0:512], bias_hh[:, :], ALU.add).then_inc(prep_w, 1)
            dve.wait_ge(prep_w, 4)
            zc = bias[:, 0:512].rearrange("p (a c) -> p a c", c=256)[:, :, D:2 * D]
            dve.tensor_scalar(zc, zc, -1.0, None, ALU.mult).then_inc(prep_w, 1)
            dve.wait_ge(prep_w, 5)
            dve.tensor_copy(bias_hi[:, :], bias[:, :]).then_inc(prep_w, 1)
            dve.wait_ge(prep_w, 6)
            dve.tensor_tensor(bias_r1[:, :], bias[:, :], bias_hi[:, :], ALU.subtract).then_inc(prep_w, 1)
            dve.wait_ge(prep_w, 7)
            dve.tensor_copy(bias_mid[:, :], bias_r1[:, :]).then_inc(prep_w, 1)
            dve.wait_ge(prep_w, 8)
            dve.tensor_tensor(bias_r2[:, :], bias_r1[:, :], bias_mid[:, :], ALU.subtract).then_inc(prep_w, 1)
            dve.wait_ge(prep_w, 9)
            dve.tensor_copy(bias_lo[:, :], bias_r2[:, :]).then_inc(prep_w, 1)
            dve.wait_ge(prep_w, 10)
            dve.tensor_copy(bias3[0:1, :], bias_hi[0:1, :])
            dve.tensor_copy(bias3[32:33, :], bias_mid[32:33, :])
            dve.tensor_copy(bias3[64:65, :], bias_lo[64:65, :]).then_inc(ready, 1)

            def build_same(ph, b):
                dve.wait_ge(in_keys.sem(b), in_keys.at(ph, b))
                if (b - 2).real:
                    dve.wait_ge(d_mm.sem, d_mm.at(ph, b - 2))
                a = 0 if ph < 2 else TILES
                dve.tensor_tensor(same[b.p][:, a:EG, :], groups(keyr[b.p], a, EG - a, P),
                                  keyc[b.p][:, a:EG].unsqueeze(2).broadcast_to([P, EG - a, P]), ALU.is_equal
                                  ).then_inc(s_built.sem, 1)

            def center(ph, b):
                n = updated[ph]
                dve.wait_ge(sum_done.sem, sum_done.at(ph, b))
                v = groups(y[b.p], 0, n)
                dve.scalar_tensor_tensor(v, spread(tot, n), -1.0 / D, v, ALU.mult, ALU.add).then_inc(cen_done.sem, 1)

            def row_sums(ph, b):
                dve.wait_ge(y_done.sem, y_done.at(ph, b, y_done.per[ph] - 1))
                n = updated[ph]
                dve.tensor_reduce(tot[:, 0:n], groups(y[b.p], 0, n), AX_X, ALU.add).then_inc(sum_done.sem, 1)

            def square_sums(ph, b):
                dve.wait_ge(sq_done.sem, sq_done.at(ph, b))
                n = updated[ph]
                dve.tensor_reduce(ssq[:, 0:n], groups(sq[b.p], 0, n), AX_X, ALU.add).then_inc(ssq_done.sem, 1)

            def newton_step(ph, b, k):
                n = updated[ph]
                if k == 0:
                    dve.wait_ge(ssq_done.sem, ssq_done.at(ph, b))
                else:
                    dve.wait_ge(newton.sem, newton.at(ph, b, k - 1))
                r = rinv_i[:, 0:n].bitcast(F32)
                if k == 0:
                    i = dve.tensor_scalar(var[:, 0:n], ssq[:, 0:n], 1.0 / D, EPS, ALU.mult, ALU.add)
                elif k == 1:
                    i = dve.tensor_scalar(seed[:, 0:n], var[:, 0:n].bitcast(I32), 1, None, ALU.logical_shift_right)
                elif k == 2:
                    i = dve.tensor_scalar(rinv_i[:, 0:n], seed[:, 0:n], -1.0, RSQRT_SEED, ALU.mult, ALU.add)
                elif k % 3 == 0:
                    i = dve.tensor_tensor(nt_a[:, 0:n], r, r, ALU.mult)
                elif k % 3 == 1:
                    i = dve.scalar_tensor_tensor(nt_b[:, 0:n], nt_a[:, 0:n], -0.5, var[:, 0:n], ALU.mult, ALU.mult)
                else:
                    i = dve.scalar_tensor_tensor(r, nt_b[:, 0:n], 1.5, r, ALU.add, ALU.mult)
                i.then_inc(newton.sem, 1)

            def scale(ph, b):
                n = updated[ph]
                dve.wait_ge(newton.sem, newton.at(ph, b, NEWTON - 1))
                if (b - 2).real:
                    dve.wait_ge(st_x.sem(b), st_x.at(ph, b - 2))
                    if ph < 3:
                        dve.wait_ge(st_ends.sem(b), st_ends.at(ph, b - 2))
                    if ph < 4:
                        dve.wait_ge(e_trans.sem, e_trans.at(ph, b - 2))
                m = NG if ph == 3 else n
                i = dve.tensor_tensor(groups(xn[b.p], 0, m), groups(y[b.p], 0, m), spread(rinv, m), ALU.mult)
                if ph == 3:
                    i = dve.tensor_tensor(groups(xn[b.p], NG, EG)[:, 0:EG:2, :], groups(y[b.p], NG, TILES),
                                          rinv[:, NG:n].unsqueeze(2).broadcast_to([P, TILES, D]), ALU.mult)
                i.then_inc(ln_done.sem, 1)

            rinv = rinv_i[:, :].bitcast(F32)

            def body0(b):
                build_same(0, b)
                if (b - 2).real:
                    dve.wait_ge(st_rows.sem(b), st_rows.at(0, b - 2))
                    dve.wait_ge(dst_added, dst_at(0, b - 2, 1))
                dve.tensor_copy(key_f[:, :], keyc[b.p][:, :]).then_inc(prep.sem, 1)
                dve.wait_ge(s_built.sem, s_built.at(0, b))
                dve.tensor_tensor(earlier[:, :, :], same[b.p][:, :, :], before[:, :].unsqueeze(1).broadcast_to([P, EG, P]),
                                  ALU.mult).then_inc(prep.sem, 1)
                dve.wait_ge(prep.sem, prep.at(0, b, 1))
                dve.tensor_reduce(dup[:, :], earlier[:, :, :], AX_X, ALU.add).then_inc(prep.sem, 1)
                dve.tensor_tensor(off[:, :], spare[:, :], key_f[:, :], ALU.subtract).then_inc(prep.sem, 1)
                dve.wait_ge(prep.sem, prep.at(0, b, 3))
                dve.tensor_scalar(dup1[:, :], dup[:, :], 1.0, None, ALU.min).then_inc(prep.sem, 1)
                dve.wait_ge(prep.sem, prep.at(0, b, 4))
                dve.tensor_tensor(off1[:, :], off[:, :], dup1[:, :], ALU.mult).then_inc(prep.sem, 1)
                dve.wait_ge(prep.sem, prep.at(0, b, 5))
                dve.tensor_tensor(row_f[:, :], off1[:, :], key_f[:, :], ALU.add).then_inc(prep.sem, 1)
                dve.wait_ge(prep.sem, prep.at(0, b, 6))
                dve.tensor_copy(s_rows[b.p][:, 0:EG], row_f[:, :]).then_inc(prep.sem, 1)
                dve.tensor_scalar(s_rows[b.p][:, EG:EG + TILES], row_f[:, 0:TILES], 2.0, 1.0, ALU.mult, ALU.add
                                  ).then_inc(prep.sem, 1)
                dve.tensor_scalar(s_rows[b.p][:, EG + TILES:2 * EG], row_f[:, TILES:EG], 2.0, None, ALU.mult
                                  ).then_inc(prep.sem, 1)

            steps(dve, body0, 0)

            def times_r(b, k):
                dve.wait_ge(gate_done.sem, gate_done.at(1, b, k))
                if (b - 2).real:
                    dve.wait_ge(tanh_done.sem, tanh_done.at(1, b - 2))
                c = buf(1, b, k)
                g = pG[:, 2 * c:2 * c + 2, :].rearrange("p a (g c) -> p (a g) c", c=256)
                dve.tensor_tensor(groups(pre_n[b.p], k * CH, CH), groups(gates[b.p], k * CH, CH, 2 * D)[:, :, 0:D],
                                  g[:, :, 3 * D:4 * D], ALU.mult).then_inc(rn_done.sem, 1)

            def plus_n(b, k):
                dve.wait_ge(rn_done.sem, rn_done.at(1, b, k))
                c = buf(1, b, k)
                g = pG[:, 2 * c:2 * c + 2, :].rearrange("p a (g c) -> p (a g) c", c=256)
                v = groups(pre_n[b.p], k * CH, CH)
                dve.tensor_tensor(v, v, g[:, :, 2 * D:3 * D], ALU.add).then_inc(g_used.sem, 1)

            def body1(s):
                f = s - 1
                if s.real:
                    times_r(s, 0)
                    times_r(s, 1)
                    plus_n(s, 0)
                    plus_n(s, 1)
                if f.real:
                    square_sums(1, f)
                    build_same(1, f)
                    newton_step(1, f, 0)
                if s.real:
                    times_r(s, 2)
                if f.real:
                    newton_step(1, f, 1)
                if s.real:
                    plus_n(s, 2)
                if f.real:
                    for k in range(2, 6):
                        newton_step(1, f, k)
                if s.real:
                    dve.wait_ge(tanh_done.sem, tanh_done.at(1, s))
                    dve.wait_ge(in_rows.sem(s), in_rows.at(1, s))
                    dve.tensor_tensor(groups(diff[s.p], 0, G), groups(act_n[s.p], 0, G), x_of(1, s, 0, G), ALU.subtract
                                      ).then_inc(diff_done.sem, 1)
                if f.real:
                    newton_step(1, f, 6)
                if s.real:
                    dve.wait_ge(diff_done.sem, diff_done.at(1, s))
                    dve.tensor_tensor(groups(diff[s.p], 0, G), groups(gates[s.p], 0, G, 2 * D)[:, :, D:2 * D],
                                      groups(diff[s.p], 0, G), ALU.mult).then_inc(zd_done.sem, 1)
                if f.real:
                    newton_step(1, f, 7)
                if s.real:
                    dve.wait_ge(zd_done.sem, zd_done.at(1, s))
                    dve.scalar_tensor_tensor(groups(y[s.p], 0, G), x_of(1, s, 0, G), 2.0, groups(diff[s.p], 0, G), ALU.mult, ALU.add
                                             ).then_inc(y_done.sem, 1)
                if f.real:
                    newton_step(1, f, 8)
                if s.real:
                    row_sums(1, s)
                if f.real:
                    newton_step(1, f, 9)
                    newton_step(1, f, 10)
                if s.real:
                    center(1, s)
                if f.real:
                    newton_step(1, f, 11)
                    scale(1, f)

            steps(dve, body1, 1)

            def add_first(b, k):
                dve.wait_ge(g_done.sem, g_done.at(2, b, k))
                sums = sums_of(2, b, k * CH, CH)
                dve.tensor_tensor(groups(diff[b.p], k * CH, CH), groups(pG[:, buf(2, b, k), :], 0, CH), sums[:, :, 0:D],
                                  ALU.add).then_inc(g_used.sem, 1)

            def body2(s):
                f = s - 1
                if s.real:
                    add_first(s, 0)
                    add_first(s, 1)
                if f.real:
                    square_sums(2, f)
                    build_same(2, f)
                    newton_step(2, f, 0)
                if s.real:
                    dve.wait_ge(gathered.sem(s), gathered.at(2, s))
                    add_first(s, 2)
                if f.real:
                    for k in range(1, 6):
                        newton_step(2, f, k)
                if s.real:
                    dve.wait_ge(g_used.sem, g_used.at(2, s, 2))
                    dve.tensor_tensor(groups(y[s.p], 0, G), groups(diff[s.p], 0, G),
                                      sums_of(2, s, 0, G)[:, :, D:2 * D], ALU.add
                                      ).then_inc(y_done.sem, 1)
                if f.real:
                    newton_step(2, f, 6)
                    newton_step(2, f, 7)
                if s.real:
                    row_sums(2, s)
                if f.real:
                    newton_step(2, f, 8)
                    newton_step(2, f, 9)
                if s.real:
                    center(2, s)
                if f.real:
                    newton_step(2, f, 10)
                    newton_step(2, f, 11)
                    scale(2, f)

            steps(dve, body2, 1)

            def means(b):
                n = updated[3]
                dve.wait_ge(in_rows.sem(b), in_rows.at(3, b))
                dve.wait_ge(gathered.sem(b), gathered.at(3, b))
                sums = sums_of(3, b, 0, n)
                dve.tensor_scalar(cnt[:, 0:n].unsqueeze(2), sums[:, :, D:D + 1], 1.0, None, ALU.max).then_inc(cnt_done.sem, 1)
                dve.wait_ge(cnt_done.sem, cnt_done.at(3, b, 0))
                dve.reciprocal(rcnt[:, 0:n], cnt[:, 0:n]).then_inc(cnt_done.sem, 1)
                dve.wait_ge(cnt_done.sem, cnt_done.at(3, b, 1))
                if (b - 2).real:
                    dve.wait_ge(t_done.sem, t_done.at(3, b - 2, 2))
                dve.tensor_tensor(groups(rows[b.p], 0, n, 2 * D)[:, :, D:2 * D], sums[:, :, 0:D], spread(rcnt, n), ALU.mult
                                  ).then_inc(pre_done.sem, 1)

            def relu_plus_x(b, k):
                dve.wait_ge(g_done.sem, g_done.at(3, b, k))
                n = min(updated[3], (k + 1) * CH) - k * CH
                dve.scalar_tensor_tensor(groups(y[b.p], k * CH, n), groups(pG[:, buf(3, b, k), :], 0, n), 0.0,
                                         x_of(3, b, k * CH, n), ALU.max, ALU.add).then_inc(y_done.sem, 1)

            def body3(s):
                f = s - 1
                if s.real:
                    means(s)
                if f.real:
                    square_sums(3, f)
                    build_same(3, f)
                    for k in range(0, 4):
                        newton_step(3, f, k)
                for k in range(3):
                    if s.real:
                        relu_plus_x(s, k)
                    if f.real:
                        newton_step(3, f, 4 + k)
                if f.real:
                    newton_step(3, f, 7)
                if s.real:
                    row_sums(3, s)
                if f.real:
                    newton_step(3, f, 8)
                    newton_step(3, f, 9)
                if s.real:
                    center(3, s)
                if f.real:
                    newton_step(3, f, 10)
                    newton_step(3, f, 11)
                    scale(3, f)

            steps(dve, body3, 1)

            def body4(s):
                f = s - 1
                if s.real:
                    dve.wait_ge(in_rows.sem(s), in_rows.at(4, s))
                    if (s - 2).real:
                        dve.wait_ge(t_done.sem, t_done.at(4, s - 2, 1))
                    r = rows[s.p]
                    dve.scalar_tensor_tensor(r[:, W:W + NG * D], r[:, 0:NG * D], eps1p[:, 0:1],
                                             r[:, RAW:RAW + NG * D], ALU.mult, ALU.add).then_inc(pre_done.sem, 1)
                if f.real:
                    square_sums(4, f)
                    for k in range(0, 8):
                        newton_step(4, f, k)
                if s.real:
                    dve.wait_ge(g_used.sem, g_used.at(4, s, 1))
                    dve.tensor_tensor(y[s.p][:, 0:NG * D], act_n[s.p][:, 0:NG * D], rows[s.p][:, 0:NG * D], ALU.add
                                      ).then_inc(y_done.sem, 1)
                if f.real:
                    newton_step(4, f, 8)
                if s.real:
                    row_sums(4, s)
                if f.real:
                    newton_step(4, f, 9)
                    newton_step(4, f, 10)
                if s.real:
                    center(4, s)
                if f.real:
                    newton_step(4, f, 11)
                    scale(4, f)

            steps(dve, body4, 1)


def kernel(**inputs):
    import numpy as np
    import concourse.bacc as bacc
    from concourse.bass_utils import run_bass_kernel_spmd

    a = {k: np.asarray(v) for k, v in inputs.items()}
    slots = PAIRS * TILES

    def by_tile(v, pad):
        full = np.full((P * slots,) + v.shape[1:], pad, v.dtype)
        full[:E] = v
        return full.reshape((P, PAIRS, TILES) + v.shape[1:])

    def both(pad):
        ends = np.stack([by_tile(a["src"], pad), by_tile(a["dst"], pad)], axis=2)
        return np.ascontiguousarray(ends.transpose(1, 0, 2, 3).reshape(PAIRS, P, EG))

    arrays = {
        "x": a["x"],
        "gather_rows": both(0),
        "key_cols": both(N),
        "key_rows": np.ascontiguousarray(both(N).transpose(0, 2, 1).reshape(PAIRS, EG * P)),
        "attr_rows": np.ascontiguousarray(
            by_tile(a["edge_weight1"][:, 0], 0).transpose(1, 2, 0).reshape(PAIRS, TILES * P)),
        "attr64": by_tile(a["edge_attr_64"], 0).reshape(P, PAIRS, TILES * D),
    }
    turned = ("L0_gnn_W1", "L0_gnn_W2", "L0_gnn_W_ih", "L0_gnn_W_hh", "L1_gnn_w0_w", "L1_gnn_w1_w")
    for k, v in a.items():
        if k.startswith("L"):
            arrays[k.replace("_gnn", "")] = np.ascontiguousarray(v.T) if k in turned else v

    nc = bacc.Bacc("TRN2", target_bir_lowering=False, num_devices=1)
    t = {k: nc.dram_tensor(k, v.shape, mybir.dt.from_np(v.dtype), kind="ExternalInput").ap() for k, v in arrays.items()}
    out = nc.dram_tensor("new_x", (N, D), F32, kind="ExternalOutput").ap()
    build(nc, t["x"], t["gather_rows"], t["key_cols"], t["key_rows"], t["attr_rows"], t["attr64"], t, out)
    r = run_bass_kernel_spmd(nc, [arrays], core_ids=[0])
    return r.results[0]["new_x"]
```

```python
from contextlib import ExitStack

import concourse.bass as bass
from concourse import mybir

F32 = mybir.dt.float32
BF16 = mybir.dt.bfloat16
I32 = mybir.dt.int32
ALU = mybir.AluOpType
ACT = mybir.ActivationFunctionType
AX_X = mybir.AxisListType.X

P = 128
N, D, E = 100000, 64, 25000
NODES = 1024
NG = NODES // P
TILES = 2
EG = 2 * TILES
G = NG + EG
PAIRS = -(-N // NODES)
ROWS = PAIRS * NODES
assert PAIRS * TILES * P >= E and ROWS - N > P
W = G * D
RAW = 2 * W
CH = 4
EPS = 1e-5
RSQRT_SEED = float(0x5F3759DF)
PHASES = 5
CHUNKS = {1: 3, 2: 3, 3: 3, 4: 2}
LAST_ROWS = N - (PAIRS - 1) * NODES
LAST_P = LAST_ROWS // NG
assert LAST_P * NG == LAST_ROWS
NEWTON = 12
SLOTS = 4
SCATTER_SKEW = {0: 3, 1: 4, 2: 4, 3: 5}
STORE_SKEW = {1: 4, 2: 4, 3: 4, 4: 4}
WEIGHT_DMAS = 45


class Pair:

    def __init__(self, c, reg=None):
        self.c, self.reg = c, reg
        self.p = c % 2
        self.q = c % SLOTS

    def __sub__(self, k):
        return Pair(self.c - k, self.reg)

    def __add__(self, k):
        return Pair(self.c + k, self.reg)

    def times(self, m, add):
        n = m * self.c + add
        return n if self.reg is None else self.reg * (SLOTS * m) + n

    def rounds(self, m, add):
        n = m * (self.c // SLOTS) + add
        return n if self.reg is None else self.reg * m + n

    @property
    def real(self):
        return self.reg is not None or 0 <= self.c < PAIRS

    @property
    def index(self):
        return self.c if self.reg is None else self.reg * SLOTS + self.c


def steps(eng, body, skew, ahead=0):
    total = PAIRS + skew
    lead = -(-(skew + SLOTS) // SLOTS) * SLOTS
    tail = skew + max(1, ahead)
    tail += (total - lead - tail) % SLOTS
    for s in range(lead):
        body(Pair(s))
    with eng.Fori(0, (total - lead - tail) // SLOTS) as i:
        for k in range(SLOTS):
            body(Pair(lead + k, i))
    for s in range(total - tail, total):
        body(Pair(s))


class Event:

    def __init__(self, sem, per):
        self.sem, self.per = sem, per

    def end(self, ph):
        return sum(PAIRS * n for q, n in self.per.items() if q < ph)

    def at(self, ph, b, k=0):
        return b.times(self.per[ph], self.end(ph) + k + 1)


class Landed:

    def __init__(self, sems, per):
        self.sems, self.per = sems, per

    def sem(self, b):
        return self.sems[b.q]

    def end(self, ph, q):
        return sum(16 * n * len(range(q, PAIRS, SLOTS)) for f, n in self.per.items() if f < ph)

    def at(self, ph, b):
        n = 16 * self.per[ph]
        return b.rounds(n, self.end(ph, b.q) + n)


def build(nc, x_in, gather_rows, key_cols, key_rows, attr_rows, attr64, weights, out):
    w = weights
    dram = lambda name, shape, dt: nc.dram_tensor(name, shape, dt, kind="Internal").ap()
    x_dram = dram("x_nodes", [ROWS, D], F32)
    ends_dram = dram("x_edge_ends", [PAIRS, P, EG * D], F32)
    rows_dram = dram("scatter_rows", [PAIRS, P, 2 * EG], I32)
    table = [dram("sums0", [ROWS, D], F32), dram("sums1", [ROWS, 2 * D], F32),
             dram("sums2", [ROWS, D + 1], F32), dram("sums3", [ROWS, D], F32)]
    width = [D, 2 * D, D + 1, D]
    halves1 = table[1].rearrange("n (h d) -> (n h) d", h=2)

    def nodes_of(t):
        return t.rearrange("(b p r) d -> b p (r d)", p=P, r=NG)

    with ExitStack() as ctx:
        def sb(name, shape, dt=F32):
            return ctx.enter_context(nc.sbuf_tensor(name, shape, dt))

        def ps(name, shape):
            return ctx.enter_context(nc.psum_tensor(name, shape, F32))

        def sem(name):
            return ctx.enter_context(nc.semaphore(name))

        def event(name, per):
            return Event(sem(name), per)

        def landed(name, per):
            return Landed([sem(f"{name}_{q}") for q in range(SLOTS)], per)

        ident = sb("ident", [P, P])
        before = sb("before", [P, P])
        spare = sb("spare", [P, EG])
        spare_i = sb("spare_i", [P, EG], I32)
        zeros = sb("zeros", [P, 2 * NG * D])
        w_gru = sb("w_gru", [P, 4 * D])
        w_h = sb("w_h", [P, 2 * D])
        w_e = sb("w_e", [1, 2 * D])
        b_h = sb("b_h", [P, 1])
        w_m0 = sb("w_m0", [P, D])
        w_self = sb("w_self", [P, 2 * D])
        w_nb = sb("w_nb", [P, 2 * D])
        w_m2 = sb("w_m2", [P, D])
        w_u2 = sb("w_u2", [P, D])
        w_m3 = sb("w_m3", [P, D])
        w_u3 = sb("w_u3", [P, 2 * D])
        eps_col = sb("eps_col", [P, 1])
        eps1 = sb("eps1", [P, 1])
        eps1p = sb("eps1p", [P, 1])
        BIAS = {"gru": (0, 512), "m0": (512, 128), "self": (640, 256), "nb": (896, 256), "m2": (1152, 128),
                "u2": (1280, 256), "m3": (1536, 128), "u3": (1664, 256)}
        NB = 1920
        bias = sb("bias", [65, NB])
        bias_hh = sb("bias_hh", [65, 512])
        bias_hi = sb("bias_hi", [65, NB], BF16)
        bias_mid = sb("bias_mid", [65, NB], BF16)
        bias_lo = sb("bias_lo", [65, NB], BF16)
        bias_r1 = sb("bias_r1", [65, NB])
        bias_r2 = sb("bias_r2", [65, NB])
        bias3 = sb("bias3", [65, NB], BF16)
        ones65 = sb("ones65", [65, P], BF16)

        two = range(2)
        rows = [sb(f"rows{p}", [P, 4 * W]) for p in range(SLOTS)]
        g_rows = [sb(f"g_rows{p}", [P, EG], I32) for p in range(SLOTS)]
        s_rows = [sb(f"s_rows{p}", [P, 2 * EG], I32) for p in range(SLOTS)]
        keyc = [sb(f"keyc{p}", [P, EG], I32) for p in range(SLOTS)]
        keyr = [sb(f"keyr{p}", [P, EG * P], I32) for p in range(SLOTS)]
        attr_r = [sb(f"attr_r{p}", [1, TILES * P]) for p in range(SLOTS)]
        xt = [sb(f"xt{p}", [P, CH * P]) for p in two]
        gates = [sb(f"gates{p}", [P, G * 2 * D]) for p in two]
        pre_n = [sb(f"pre_n{p}", [P, W]) for p in two]
        act_n = [sb(f"act_n{p}", [P, W]) for p in two]
        diff = [sb(f"diff{p}", [P, W]) for p in two]
        y = [sb(f"y{p}", [P, W]) for p in two]
        sq = [sb(f"sq{p}", [P, W]) for p in two]
        xn = [sb(f"xn{p}", [P, W]) for p in range(SLOTS)]
        same = [sb(f"same{p}", [P, EG, P]) for p in two]
        earlier = sb("earlier", [P, EG, P])
        et = [sb(f"et{p}", [P, TILES * P]) for p in two]
        hid = [sb(f"hid{p}", [P, TILES * P]) for p in two]
        msg = [sb(f"msg{p}", [P, 4 * D + 2]) for p in two]
        summed = [sb(f"summed{p}", [P, EG * (D + 1)]) for p in range(SLOTS)]
        tot = sb("tot", [P, G])
        ssq = sb("ssq", [P, G])
        var = sb("var", [P, G])
        seed = sb("seed", [P, G], I32)
        rinv_i = sb("rinv_i", [P, G], I32)
        nt_a = sb("nt_a", [P, G])
        nt_b = sb("nt_b", [P, G])
        std = sb("std", [P, G])
        cnt = sb("cnt", [P, G])
        rcnt = sb("rcnt", [P, G])
        key_f = sb("key_f", [P, EG])
        dup = sb("dup", [P, EG])
        dup1 = sb("dup1", [P, EG])
        off = sb("off", [P, EG])
        off1 = sb("off1", [P, EG])
        row_f = sb("row_f", [P, EG])

        pT = ps("pT", [P, 2, 512])
        pG = ps("pG", [P, 4, 512])
        pEM = ps("pEM", [P, 512])
        pE, pM = pEM[:, 0:256], pEM[:, 256:512]
        pD = ps("pD", [P, 512])

        w_landed = sem("w_landed")
        zero0 = sem("zero0")
        zeroed = landed("zeroed", {0: 1, 1: 1, 2: 1})
        in_rows = landed("in_rows", {1: 3, 2: 3, 3: 3, 4: 2})
        in_gidx = landed("in_gidx", {0: 1, 1: 1, 2: 1, 3: 1})
        in_keys = landed("in_keys", {0: 3, 1: 2, 2: 2, 3: 2})
        in_sidx = landed("in_sidx", {1: 1, 2: 1, 3: 1})
        in_attr = landed("in_attr", {3: 1})
        gathered = landed("gathered", {0: 4, 1: 4, 2: 4, 3: 2})
        st_x = landed("st_x", {1: 1, 2: 1, 3: 1, 4: 1})
        st_ends = landed("st_ends", {0: 1, 1: 1, 2: 1})
        st_rows = landed("st_rows", {0: 1})
        dst_added = sem("dst_added")
        src_added = sem("src_added")

        ready = sem("ready")
        pool_ready = sem("pool_ready")
        held = [sem("held_sp"), sem("held_pool")]
        prep_w = sem("prep_w")
        e03 = {0: 1, 1: 1, 2: 1, 3: 1}
        u14 = {1: 1, 2: 1, 3: 1, 4: 1}
        t_done = event("t_done", CHUNKS)
        t_copied = event("t_copied", CHUNKS)
        g_done = event("g_done", CHUNKS)
        g_used = event("g_used", {1: 3, 2: 3, 4: 2})
        gate_done = event("gate_done", {1: 3})
        rn_done = event("rn_done", {1: 3})
        tanh_done = event("tanh_done", {1: 1})
        diff_done = event("diff_done", {1: 1})
        zd_done = event("zd_done", {1: 1})
        cnt_done = event("cnt_done", {3: 2})
        pre_done = event("pre_done", {3: 1, 4: 1})
        gelu_done = event("gelu_done", {4: 2})
        y_done = event("y_done", {1: 1, 2: 1, 3: 3, 4: 1})
        sum_done = event("sum_done", u14)
        cen_done = event("cen_done", u14)
        sq_done = event("sq_done", u14)
        ssq_done = event("ssq_done", u14)
        std_done = event("std_done", {2: 1})
        newton = event("newton", {1: NEWTON, 2: 1, 3: NEWTON, 4: NEWTON})
        ln_done = event("ln_done", u14)
        e_trans = event("e_trans", e03)
        e_copied = event("e_copied", e03)
        h_mm = event("h_mm", {0: 1})
        h_act = event("h_act", {0: 1})
        m_mm = event("m_mm", e03)
        m_act = event("m_act", e03)
        s_built = event("s_built", e03)
        prep = event("prep", {0: 10})
        d_mm = event("d_mm", e03)
        d_act = event("d_act", e03)

        def hold(eng):
            eng.sem_inc(held[eng is nc.gpsimd], 1)

        def dst_at(ph, b, t):
            return b.times(32, 32 * PAIRS * ph + 16 * (t + 1))

        def src_at(b, t):
            return b.times(32, 16 * (t + 1))

        def bias_of(name, n=None):
            a, m = BIAS[name]
            return bias3[:, a:a + (n or m)]

        def buf(ph, b, k):
            return (CHUNKS[ph] * b.p + k) % 2

        def groups(t, a, n, c=D):
            return t[:, a * c:(a + n) * c].rearrange("p (g c) -> p g c", c=c)

        def spread(t, n, c=D):
            return t[:, 0:n].unsqueeze(2).broadcast_to([P, n, c])

        def x_of(ph, b, a, n):
            if ph in (1, 3):
                return groups(rows[b.q], a, n, 2 * D)[:, :, 0:D]
            return groups(rows[b.q], a, n)

        def sums_of(ph, b, a, n):
            if ph == 1:
                return groups(rows[b.q], a, n, 2 * D)[:, :, D:2 * D]
            return groups(rows[b.q][:, RAW:4 * W], a, n, width[ph - 1])

        updated = {1: G, 2: G, 3: NG + TILES, 4: NG}

        block = ctx.enter_context(nc.Block())

        @block.sync
        def _(sp):
            def put(dst, src):
                sp.dma_start(dst, src).then_inc(w_landed, 16)
                return 16

            sp.wait_ge(ready, 2)
            put(w_gru[0:D, 0:2 * D], w["L0_W_hh"][:, 0:2 * D])
            put(w_gru[0:D, 3 * D:4 * D], w["L0_W_hh"][:, 2 * D:3 * D])
            put(w_gru[D:P, 0:3 * D], w["L0_W_ih"])
            put(w_h[:, :], w["L0_W1"][0:P, :])
            put(w_e[:, :], w["L0_W1"][P:P + 1, :])
            put(b_h[:, :], w["L0_b1"].rearrange("(p o) -> p o", o=1))
            put(w_m0[:, :], w["L0_W2"])
            for dst, name in ((w_self, "L1_w0_w"), (w_nb, "L1_w1_w"), (w_u3, "L3_W_upd")):
                put(dst[0:D, 0:D], w[name])
                put(dst[D:P, D:P], w[name])
            put(w_m2[:, :], w["L2_W_msg"])
            put(w_u2[:, :], w["L2_W_upd"])
            put(w_m3[:, :], w["L3_W_msg"])
            put(eps1[:, :], w["L3_eps"].unsqueeze(0).broadcast_to([P, 1]))
            for rep in range(2):
                put(bias[:, rep * 256:rep * 256 + 3 * D], w["L0_b_ih"].unsqueeze(0).broadcast_to([65, 3 * D]))
                put(bias_hh[:, rep * 256:rep * 256 + 2 * D], w["L0_b_hh"][0:2 * D].unsqueeze(0).broadcast_to([65, 2 * D]))
                put(bias_hh[:, rep * 256 + 3 * D:rep * 256 + 4 * D],
                    w["L0_b_hh"][2 * D:3 * D].unsqueeze(0).broadcast_to([65, D]))
            for name, src in (("m0", "L0_b2"), ("self", "L1_w0_b"), ("nb", "L1_w1_b"), ("m2", "L2_b_msg"),
                              ("u2", "L2_b_upd"), ("m3", "L3_b_msg"), ("u3", "L3_b_upd")):
                a, m = BIAS[name]
                for c in range(a, a + m, D):
                    put(bias[:, c:c + D], w[src].unsqueeze(0).broadcast_to([65, D]))

            def load_gidx(ph, b):
                if (b - SLOTS).real:
                    sp.wait_ge(gathered.sem(b), gathered.at(ph, b - SLOTS))
                hold(sp)
                sp.dma_start(g_rows[b.q][:, :], gather_rows[b.index]).then_inc(in_gidx.sem(b), 16)

            def next_gidx(ph, s):
                if s.reg is None and s.c == 0:
                    load_gidx(ph, s)
                if (s + 1).real:
                    load_gidx(ph, s + 1)

            def load_keys(ph, b):
                if (b - SLOTS).real:
                    sp.wait_ge(s_built.sem, s_built.at(ph, b - SLOTS))
                    if ph == 0:
                        hold(sp)
                        sp.wait_ge(prep.sem, prep.at(0, b - SLOTS, 0))
                        hold(sp)
                        sp.wait_ge(h_mm.sem, h_mm.at(0, b - SLOTS))
                hold(sp)
                first = 0 if ph < 2 else TILES
                sp.dma_start(keyr[b.q][:, first * P:EG * P],
                             key_rows[b.index][first * P:EG * P].unsqueeze(0).broadcast_to([P, (EG - first) * P])
                             ).then_inc(in_keys.sem(b), 16)
                sp.dma_start(keyc[b.q][:, :], key_cols[b.index]).then_inc(in_keys.sem(b), 16)
                if ph == 0:
                    sp.dma_start(attr_r[b.q][:, :], attr_rows[b.index].unsqueeze(0)).then_inc(in_keys.sem(b), 16)

            def zero(ph, b):
                n = NG * width[ph + 1]
                sp.dma_start(nodes_of(table[ph + 1])[b.index], zeros[:, 0:n]).then_inc(zeroed.sem(b), 16)

            def load_rows(ph, b, last=False):
                if (b - SLOTS).real:
                    sp.wait_ge(y_done.sem, y_done.at(ph, b - SLOTS, y_done.per[ph] - 1))
                hold(sp)
                if ph > 1:
                    x, to = x_dram, x_of(ph, b, 0, NG)
                    src = x[:, :].rearrange("(b p r) d -> b p r d", p=P, r=NG)[b.index]
                elif last:
                    to = x_of(1, b, 0, NG)[0:LAST_P]
                    src = x_in[(PAIRS - 1) * NODES:N, :].rearrange("(p r) d -> p r d", r=NG)
                else:
                    to = x_of(1, b, 0, NG)
                    src = x_in[0:(PAIRS - 1) * NODES, :].rearrange("(b p r) d -> b p r d", p=P, r=NG)[b.index]
                sp.dma_start(to, src).then_inc(in_rows.sem(b), 16)
                sp.dma_start(sums_of(ph, b, 0, NG),
                             table[ph - 1].rearrange("(b p r) d -> b p r d", p=P, r=NG)[b.index]
                             ).then_inc(in_rows.sem(b), 16)
                if ph < 4:
                    m = updated[ph] - NG
                    ends = ends_dram[b.index].rearrange("p (g c) -> p g c", c=D)
                    sp.dma_start(x_of(ph, b, NG, m), ends if ph < 3 else ends[:, 0:EG:2, :]
                                 ).then_inc(in_rows.sem(b), 16)

            def load_sidx(ph, b):
                if (b - SLOTS).real:
                    sp.wait_ge(dst_added, dst_at(ph, b - SLOTS, 1))
                    if ph == 1:
                        hold(sp)
                        sp.wait_ge(src_added, src_at(b - SLOTS, 1))
                hold(sp)
                sp.dma_start(s_rows[b.q][:, :], rows_dram[b.index]).then_inc(in_sidx.sem(b), 16)

            def load_attr(b):
                if (b - SLOTS).real:
                    sp.wait_ge(e_trans.sem, e_trans.at(3, b - SLOTS))
                hold(sp)
                sp.dma_start(groups(xn[b.q], NG, EG)[:, 1:EG:2, :],
                             attr64[:, b.index, :].rearrange("p (t c) -> p t c", c=D)).then_inc(in_attr.sem(b), 16)

            def store(ph, b, last=False):
                sp.wait_ge(ln_done.sem, ln_done.at(ph, b))
                hold(sp)
                v = xn[b.q]
                if ph < 4:
                    sp.dma_start(nodes_of(x_dram)[b.index], v[:, 0:NG * D]).then_inc(st_x.sem(b), 16)
                elif last:
                    sp.dma_start(out[(PAIRS - 1) * NODES:N, :].rearrange("(p r) d -> p (r d)", r=NG),
                                 v[0:LAST_P, 0:NG * D]).then_inc(st_x.sem(b), 16)
                else:
                    sp.dma_start(nodes_of(out[0:(PAIRS - 1) * NODES, :])[b.index], v[:, 0:NG * D]
                                 ).then_inc(st_x.sem(b), 16)
                if ph < 3:
                    sp.dma_start(ends_dram[b.index], v[:, NG * D:G * D]).then_inc(st_ends.sem(b), 16)

            def body0(s):
                next_gidx(0, s)
                if s.real:
                    load_keys(0, s)
                    zero(0, s)
                b = s - 1
                if b.real:
                    sp.wait_ge(gathered.sem(b), gathered.at(0, b))
                    hold(sp)
                    sp.dma_start(ends_dram[b.index], rows[b.q][:, NG * D:G * D]).then_inc(st_ends.sem(b), 16)
                b = s - 3
                if b.real:
                    sp.wait_ge(prep.sem, prep.at(0, b, 9))
                    hold(sp)
                    sp.dma_start(rows_dram[b.index], s_rows[b.q][:, :]).then_inc(st_rows.sem(b), 16)

            steps(sp, body0, 3, ahead=2)

            for ph in range(1, PHASES):
                sp.wait_ge(dst_added, 32 * PAIRS * ph)
                if ph == 2:
                    sp.wait_ge(src_added, 32 * PAIRS)
                for q in range(SLOTS):
                    sp.wait_ge(st_ends.sems[q], st_ends.end(ph, q))
                    if ph == 1:
                        sp.wait_ge(st_rows.sems[q], st_rows.end(ph, q))
                    if ph > 1:
                        sp.wait_ge(st_x.sems[q], st_x.end(ph, q))
                    if ph < 4:
                        sp.wait_ge(zeroed.sems[q], zeroed.end(ph, q))

                def body(s, ph=ph):
                    last = s.reg is None and s.c == PAIRS - 1
                    if ph < 4:
                        next_gidx(ph, s)
                    if s.real:
                        load_rows(ph, s, last)
                        if ph < 4:
                            load_keys(ph, s)
                        if ph == 3:
                            load_attr(s)
                    if ph < 4 and (s - 3).real:
                        load_sidx(ph, s - 3)
                    b = s - STORE_SKEW[ph]
                    if b.real:
                        store(ph, b, b.reg is None and b.c == PAIRS - 1)
                        if ph < 3:
                            zero(ph, b)

                steps(sp, body, STORE_SKEW[ph], ahead=2)
            for q in range(SLOTS):
                sp.wait_ge(st_x.sems[q], st_x.end(PHASES, q))

        @block.gpsimd
        def _(pool):
            pool.memset(ident[:, :], 0.0).then_inc(pool_ready, 1)
            pool.memset(before[:, :], 1.0).then_inc(pool_ready, 1)
            pool.wait_ge(pool_ready, 2)
            pool.affine_select(out=ident[:, :], in_=ident[:, :], compare_op=ALU.not_equal, fill=1.0, base=0,
                               pattern=[[-1, P]], channel_multiplier=1).then_inc(pool_ready, 1)
            pool.affine_select(out=before[:, :], in_=before[:, :], compare_op=ALU.is_gt, fill=0.0, base=0,
                               pattern=[[-1, P]], channel_multiplier=1).then_inc(pool_ready, 1)
            pool.iota(spare_i[:, :], pattern=[[0, EG]], base=N + 1, channel_multiplier=1).then_inc(pool_ready, 1)

            def gather(ph, b, j):
                src = x_in if ph == 0 else table[ph - 1]
                to = x_of(0, b, NG + j, 1) if ph == 0 else sums_of(ph, b, NG + j, 1)
                col = j if ph == 3 else (j % 2) * TILES + j // 2
                pool.indirect_dma_start(to[:, 0, :], None, src,
                                        bass.IndirectOffsetOnAxis(g_rows[b.q][:, col:col + 1], 0)
                                        ).then_inc(gathered.sem(b), 16)

            def may_gather(ph, b):
                pool.wait_ge(in_gidx.sem(b), in_gidx.at(ph, b))
                if not (b - SLOTS).real:
                    return
                if ph == 0:
                    pool.wait_ge(e_trans.sem, e_trans.at(0, b - SLOTS))
                    pool.wait_ge(st_ends.sem(b), st_ends.at(0, b - SLOTS))
                elif ph == 1:
                    pool.wait_ge(t_done.sem, t_done.at(1, b - SLOTS, 2))
                elif ph == 2:
                    pool.wait_ge(y_done.sem, y_done.at(2, b - SLOTS))
                else:
                    pool.wait_ge(pre_done.sem, pre_done.at(3, b - SLOTS))

            def scatter(ph, b, t):
                if t == 0:
                    pool.wait_ge(d_act.sem, d_act.at(ph, b))
                    if ph:
                        pool.wait_ge(in_sidx.sem(b), in_sidx.at(ph, b))
                    else:
                        pool.wait_ge(prep.sem, prep.at(0, b, 9))
                first = b.reg is None and b.c == 0 and t == 0
                if not first:
                    pool.wait_ge(dst_added, dst_at(ph, b, t - 1))
                n = D + 1 if ph == 2 else D
                dst = halves1 if ph == 1 else table[ph]
                hold(pool)
                col = TILES + t + (EG if ph == 1 else 0)
                at = (TILES + t) * D if ph == 1 else t * n
                pool.indirect_dma_start(dst, bass.IndirectOffsetOnAxis(s_rows[b.q][:, col:col + 1], 0),
                                        summed[b.q][:, at:at + n], None, compute_op=ALU.add).then_inc(dst_added, 16)
                if ph == 1:
                    if not first:
                        pool.wait_ge(src_added, src_at(b, t - 1))
                    hold(pool)
                    col = t + EG
                    pool.indirect_dma_start(dst, bass.IndirectOffsetOnAxis(s_rows[b.q][:, col:col + 1], 0),
                                            summed[b.q][:, t * D:(t + 1) * D], None, compute_op=ALU.add
                                            ).then_inc(src_added, 16)

            for ph in range(4):
                if ph == 0:
                    pool.wait_ge(zero0, 16)
                else:
                    for q in range(SLOTS):
                        pool.wait_ge(zeroed.sems[q], zeroed.end(ph, q))
                    pool.wait_ge(dst_added, 32 * PAIRS * ph)
                    if ph == 2:
                        pool.wait_ge(src_added, 32 * PAIRS)
                skew = SCATTER_SKEW[ph]

                def body(s, ph=ph, skew=skew):
                    b = s - skew
                    m = TILES if ph == 3 else EG
                    if s.real:
                        may_gather(ph, s)
                    for t in range(TILES):
                        if b.real:
                            scatter(ph, b, t)
                        if s.real:
                            for j in range(t * m // 2, (t + 1) * m // 2):
                                gather(ph, s, j)

                steps(pool, body, skew)
            pool.wait_ge(dst_added, 32 * PAIRS * 4)

        @block.tensor
        def _(pe):
            pe.wait_ge(pool_ready, 5)
            pe.wait_ge(ready, 3)

            def transpose_chunk(ph, b, k):
                last = min(updated[ph], (k + 1) * CH)
                if k == 0:
                    pe.wait_ge(in_rows.sem(b), in_rows.at(ph, b))
                    if ph > 2:
                        pe.wait_ge(pre_done.sem, pre_done.at(ph, b))
                if k == 2 and ph == 1:
                    pe.wait_ge(gathered.sem(b), gathered.at(ph, b))
                c = buf(ph, b, k)
                if b.reg is not None or CHUNKS[ph] * b.c + k >= 2:
                    pe.wait_ge(t_copied.sem, t_copied.at(ph, b, k - 2))
                per = 1 if ph in (1, 3) else 2
                a = W if ph == 4 else 0
                for i, g in enumerate(range(k * CH, last, per)):
                    at = a + g * P // per
                    t = pe.transpose(pT[:, c, i * P:(i + 1) * P], rows[b.q][:, at:at + P], ident[:, :])
                t.then_inc(t_done.sem, 1)

            def update_chunk(ph, b, k):
                pe.wait_ge(t_copied.sem, t_copied.at(ph, b, k))
                c = buf(ph, b, k)
                if b.reg is not None or CHUNKS[ph] * b.c + k >= 2:
                    used = y_done if ph == 3 else g_used
                    pe.wait_ge(used.sem, used.at(ph, b, k - 2))
                n = min(updated[ph], (k + 1) * CH) - k * CH
                x = xt[c]
                if ph == 1:
                    for g in range(n):
                        o = pG[:, 2 * c + g // 2, (g % 2) * 256:(g % 2 + 1) * 256]
                        if g % 2 == 0:
                            pe.matmul(pG[:, 2 * c + g // 2, :], ones65[:, :], bias_of("gru"), start=True, stop=False)
                        m = pe.matmul(o, x[:, g * P:(g + 1) * P], w_gru[:, :], start=False, stop=(g % 2 == 1))
                else:
                    name = {2: "self", 3: "u2", 4: "u3"}[ph]
                    wt = {2: w_self, 3: w_u2, 4: w_u3}[ph]
                    per = D if ph == 3 else 2 * D
                    pe.matmul(pG[:, c, 0:n * D], ones65[:, :], bias_of(name, n * D), start=True, stop=False)
                    for i in range(n * D // per):
                        m = pe.matmul(pG[:, c, i * per:(i + 1) * per], x[:, i * P:(i + 1) * P], wt[:, :],
                                      start=False, stop=(i == n * D // per - 1))
                m.then_inc(g_done.sem, 1)

            def edge_transpose(ph, b):
                if ph == 0:
                    pe.wait_ge(gathered.sem(b), gathered.at(0, b))
                    src = rows[b.q]
                else:
                    pe.wait_ge(ln_done.sem, ln_done.at(ph, b))
                    src = xn[b.q]
                if ph == 3:
                    pe.wait_ge(in_attr.sem(b), in_attr.at(3, b))
                if (b - 1).real:
                    last = h_act if ph == 0 else m_act
                    pe.wait_ge(last.sem, last.at(ph, b - 1))
                for t in range(TILES):
                    m = pe.transpose(pE[:, t * P:(t + 1) * P], src[:, (NG + 2 * t) * D:(NG + 2 * t + 2) * D], ident[:, :])
                m.then_inc(e_trans.sem, 1)

            def hidden(b):
                pe.wait_ge(e_copied.sem, e_copied.at(0, b))
                pe.wait_ge(in_keys.sem(b), in_keys.at(0, b))
                pe.matmul(pM[:, 0:TILES * P], w_h[:, :], et[b.p][:, :], start=True, stop=False)
                pe.matmul(pM[:, 0:TILES * P], w_e[:, :], attr_r[b.q][:, :], start=False, stop=True).then_inc(h_mm.sem, 1)

            def messages(ph, b):
                if ph == 0:
                    pe.wait_ge(h_act.sem, h_act.at(0, b))
                else:
                    pe.wait_ge(e_copied.sem, e_copied.at(ph, b))
                if (b - 1).real:
                    pe.wait_ge(m_act.sem, m_act.at(ph, b - 1))
                src, wt, name = [(hid, w_m0, "m0"), (et, w_nb, "nb"), (et, w_m2, "m2"), (et, w_m3, "m3")][ph]
                o = pG[:, 0, :] if ph == 0 else pM
                n = 2 * D if ph == 1 else D
                pe.matmul(o[:, 0:TILES * n], ones65[:, :], bias_of(name), start=True, stop=False)
                for t in range(TILES):
                    m = pe.matmul(o[:, t * n:(t + 1) * n], src[b.p][:, t * P:(t + 1) * P], wt[:, :],
                                  start=False, stop=(t == TILES - 1))
                m.then_inc(m_mm.sem, 1)

            def sum_by_key(ph, b):
                pe.wait_ge(m_act.sem, m_act.at(ph, b))
                pe.wait_ge(s_built.sem, s_built.at(ph, b))
                if (b - 1).real:
                    pe.wait_ge(d_act.sem, d_act.at(ph, b - 1))
                v = msg[b.p]
                if ph == 1:
                    for j in range(EG):
                        a = (j % TILES) * 2 * D + (D if j < TILES else 0)
                        m = pe.matmul(pD[:, j * D:(j + 1) * D], same[b.p][:, j, :], v[:, a:a + D], start=True, stop=True)
                else:
                    n = D + 1 if ph == 2 else D
                    for t in range(TILES):
                        m = pe.matmul(pD[:, t * n:(t + 1) * n], same[b.p][:, TILES + t, :], v[:, t * n:(t + 1) * n],
                                      start=True, stop=True)
                m.then_inc(d_mm.sem, 1)

            def body0(s):
                edge_transpose(0, s)
                hidden(s)
                messages(0, s)
                sum_by_key(0, s)

            steps(pe, body0, 0)

            for ph in range(1, 4):
                def body(s, ph=ph):
                    if s.real:
                        transpose_chunk(ph, s, 0)
                        transpose_chunk(ph, s, 1)
                    if (s - 3).real:
                        sum_by_key(ph, s - 3)
                    if s.real:
                        update_chunk(ph, s, 0)
                        transpose_chunk(ph, s, 2)
                        update_chunk(ph, s, 1)
                    if (s - 2).real:
                        edge_transpose(ph, s - 2)
                    if s.real:
                        update_chunk(ph, s, 2)
                    if (s - 2).real:
                        messages(ph, s - 2)

                steps(pe, body, 3)

            def body4(s):
                transpose_chunk(4, s, 0)
                transpose_chunk(4, s, 1)
                update_chunk(4, s, 0)
                update_chunk(4, s, 1)

            steps(pe, body4, 0)

        @block.scalar
        def _(act):
            act.wait_ge(ready, 1)
            n = PAIRS // 2
            act.dma_start(table[0].rearrange("(p k r) d -> p k (r d)", p=P, k=n),
                          zeros[:, :].unsqueeze(1).broadcast_to([P, n, 2 * NG * D])
                          ).then_inc(zero0, 16)
            act.wait_ge(ready, 3)

            def copy_chunk(ph, b, k):
                act.wait_ge(t_done.sem, t_done.at(ph, b, k))
                c = buf(ph, b, k)
                if b.reg is not None or CHUNKS[ph] * b.c + k >= 2:
                    act.wait_ge(g_done.sem, g_done.at(ph, b, k - 2))
                n = min(updated[ph], (k + 1) * CH) - k * CH
                n = n * P if ph in (1, 3) else n * D
                act.copy(xt[c][:, 0:n], pT[:, c, 0:n]).then_inc(t_copied.sem, 1)

            def gate_chunk(b, k):
                act.wait_ge(g_done.sem, g_done.at(1, b, k))
                if (b - 2).real:
                    act.wait_ge(zd_done.sem, zd_done.at(1, b - 2))
                c = buf(1, b, k)
                act.activation(groups(gates[b.p], k * CH, CH, 2 * D),
                               pG[:, 2 * c:2 * c + 2, :].rearrange("p a (g c) -> p (a g) c", c=256)[:, :, 0:2 * D],
                               ACT.Sigmoid).then_inc(gate_done.sem, 1)

            def square(ph, b):
                act.wait_ge(cen_done.sem, cen_done.at(ph, b))
                if (b - 2).real:
                    act.wait_ge(ssq_done.sem, ssq_done.at(ph, b - 2))
                n = updated[ph] * D
                act.activation(sq[b.p][:, 0:n], y[b.p][:, 0:n], ACT.Square).then_inc(sq_done.sem, 1)

            def copy_edges(ph, b):
                act.wait_ge(e_trans.sem, e_trans.at(ph, b))
                if (b - 2).real:
                    free = h_mm if ph == 0 else m_mm
                    act.wait_ge(free.sem, free.at(ph, b - 2))
                act.copy(et[b.p][:, :], pE[:, 0:TILES * P]).then_inc(e_copied.sem, 1)

            def act_messages(ph, b):
                act.wait_ge(m_mm.sem, m_mm.at(ph, b))
                if (b - 2).real:
                    act.wait_ge(d_mm.sem, d_mm.at(ph, b - 2))
                if ph == 2:
                    i = act.activation(groups(msg[b.p], 0, TILES, D + 1)[:, :, 0:D], groups(pM, 0, TILES), ACT.Relu)
                elif ph == 3:
                    i = act.activation(msg[b.p][:, 0:TILES * D], pM[:, 0:TILES * D], ACT.Gelu_apprx_tanh)
                elif ph == 1:
                    i = act.copy(msg[b.p][:, 0:TILES * 2 * D], pM[:, 0:TILES * 2 * D])
                else:
                    i = act.copy(msg[b.p][:, 0:TILES * D], pG[:, 0, 0:TILES * D])
                i.then_inc(m_act.sem, 1)

            def copy_sums(ph, b):
                act.wait_ge(d_mm.sem, d_mm.at(ph, b))
                if (b - SLOTS).real:
                    act.wait_ge(dst_added, dst_at(ph, b - SLOTS, 1))
                    if ph == 1:
                        act.wait_ge(src_added, src_at(b - SLOTS, 1))
                n = {0: TILES * D, 1: EG * D, 2: TILES * (D + 1), 3: TILES * D}[ph]
                act.copy(summed[b.q][:, 0:n], pD[:, 0:n]).then_inc(d_act.sem, 1)

            def body0(b):
                copy_edges(0, b)
                act.wait_ge(h_mm.sem, h_mm.at(0, b))
                if (b - 2).real:
                    act.wait_ge(m_mm.sem, m_mm.at(0, b - 2))
                act.activation(hid[b.p][:, :], pM[:, 0:TILES * P], ACT.Relu, bias=b_h[:, 0:1]).then_inc(h_act.sem, 1)
                act_messages(0, b)
                copy_sums(0, b)

            steps(act, body0, 0)

            for ph in range(1, 4):
                if ph == 2:
                    for q in two:
                        last = act.activation(groups(msg[q], 0, TILES, D + 1)[:, :, D:D + 1],
                                              groups(zeros, 0, TILES, D)[:, :, 0:1], ACT.Copy, bias=1.0)
                def body(s, ph=ph):
                    if s.real:
                        copy_chunk(ph, s, 0)
                        copy_chunk(ph, s, 1)
                    if (s - 3).real:
                        copy_sums(ph, s - 3)
                    if s.real:
                        if ph == 1:
                            gate_chunk(s, 0)
                        copy_chunk(ph, s, 2)
                        if ph == 1:
                            gate_chunk(s, 1)
                    if (s - 1).real:
                        square(ph, s - 1)
                    if (s - 2).real:
                        copy_edges(ph, s - 2)
                    if s.real and ph == 1:
                        gate_chunk(s, 2)
                        act.wait_ge(g_used.sem, g_used.at(1, s, 2))
                        if (s - 2).real:
                            act.wait_ge(diff_done.sem, diff_done.at(1, s - 2))
                        act.activation(act_n[s.p][:, :], pre_n[s.p][:, :], ACT.Tanh).then_inc(tanh_done.sem, 1)
                    if ph == 2 and (s - 1).real:
                        act.wait_ge(ssq_done.sem, ssq_done.at(2, s - 1))
                        if (s - 2).real:
                            act.wait_ge(newton.sem, newton.at(2, s - 2))
                        act.activation(std[:, :], ssq[:, :], ACT.Sqrt, bias=eps_col[:, 0:1], scale=1.0 / D
                                       ).then_inc(std_done.sem, 1)
                    if (s - 2).real:
                        act_messages(ph, s - 2)

                steps(act, body, 3)

            def body4(s):
                if s.real:
                    copy_chunk(4, s, 0)
                    copy_chunk(4, s, 1)
                if (s - 1).real:
                    square(4, s - 1)
                if s.real:
                    for k in range(2):
                        act.wait_ge(g_done.sem, g_done.at(4, s, k))
                        if (s - 2).real:
                            act.wait_ge(y_done.sem, y_done.at(4, s - 2))
                        act.activation(act_n[s.p][:, k * CH * D:(k + 1) * CH * D], pG[:, buf(4, s, k), 0:CH * D],
                                       ACT.Gelu_apprx_tanh).then_inc(g_used.sem, 1)

            steps(act, body4, 1)

        @block.vector
        def _(dve):
            dve.memset(zeros[:, :], 0.0).then_inc(ready, 1)
            for t in (w_gru, w_self, w_nb, w_u3, bias, bias_hh, bias3):
                dve.memset(t[:, :], 0.0)
            dve.memset(eps_col[:, :], EPS)
            dve.memset(ones65[:, :], 1.0).then_inc(ready, 1)
            dve.wait_ge(pool_ready, 5)
            dve.tensor_copy(spare[:, :], spare_i[:, :])
            dve.wait_ge(w_landed, 16 * WEIGHT_DMAS)
            dve.tensor_tensor(w_self[:, :], w_self[:, :], ident[:, :], ALU.add).then_inc(prep_w, 1)
            dve.tensor_scalar(w_gru[:, D:2 * D], w_gru[:, D:2 * D], -1.0, None, ALU.mult).then_inc(prep_w, 1)
            dve.tensor_scalar(eps1p[:, :], eps1[:, :], 1.0, None, ALU.add).then_inc(prep_w, 1)
            dve.tensor_tensor(bias[:, 0:512], bias[:, 0:512], bias_hh[:, :], ALU.add).then_inc(prep_w, 1)
            dve.wait_ge(prep_w, 4)
            zc = bias[:, 0:512].rearrange("p (a c) -> p a c", c=256)[:, :, D:2 * D]
            dve.tensor_scalar(zc, zc, -1.0, None, ALU.mult).then_inc(prep_w, 1)
            dve.wait_ge(prep_w, 5)
            dve.tensor_copy(bias_hi[:, :], bias[:, :]).then_inc(prep_w, 1)
            dve.wait_ge(prep_w, 6)
            dve.tensor_tensor(bias_r1[:, :], bias[:, :], bias_hi[:, :], ALU.subtract).then_inc(prep_w, 1)
            dve.wait_ge(prep_w, 7)
            dve.tensor_copy(bias_mid[:, :], bias_r1[:, :]).then_inc(prep_w, 1)
            dve.wait_ge(prep_w, 8)
            dve.tensor_tensor(bias_r2[:, :], bias_r1[:, :], bias_mid[:, :], ALU.subtract).then_inc(prep_w, 1)
            dve.wait_ge(prep_w, 9)
            dve.tensor_copy(bias_lo[:, :], bias_r2[:, :]).then_inc(prep_w, 1)
            dve.wait_ge(prep_w, 10)
            dve.tensor_copy(bias3[0:1, :], bias_hi[0:1, :])
            dve.tensor_copy(bias3[32:33, :], bias_mid[32:33, :])
            dve.tensor_copy(bias3[64:65, :], bias_lo[64:65, :]).then_inc(ready, 1)

            def build_same(ph, b):
                dve.wait_ge(in_keys.sem(b), in_keys.at(ph, b))
                if (b - 2).real:
                    dve.wait_ge(d_mm.sem, d_mm.at(ph, b - 2))
                a = 0 if ph < 2 else TILES
                dve.tensor_tensor(same[b.p][:, a:EG, :], groups(keyr[b.q], a, EG - a, P),
                                  keyc[b.q][:, a:EG].unsqueeze(2).broadcast_to([P, EG - a, P]), ALU.is_equal
                                  ).then_inc(s_built.sem, 1)

            def center(ph, b):
                n = updated[ph]
                dve.wait_ge(sum_done.sem, sum_done.at(ph, b))
                v = groups(y[b.p], 0, n)
                dve.scalar_tensor_tensor(v, spread(tot, n), -1.0 / D, v, ALU.mult, ALU.add).then_inc(cen_done.sem, 1)

            def row_sums(ph, b):
                dve.wait_ge(y_done.sem, y_done.at(ph, b, y_done.per[ph] - 1))
                n = updated[ph]
                dve.tensor_reduce(tot[:, 0:n], groups(y[b.p], 0, n), AX_X, ALU.add).then_inc(sum_done.sem, 1)

            def square_sums(ph, b):
                dve.wait_ge(sq_done.sem, sq_done.at(ph, b))
                n = updated[ph]
                dve.tensor_reduce(ssq[:, 0:n], groups(sq[b.p], 0, n), AX_X, ALU.add).then_inc(ssq_done.sem, 1)

            def newton_step(ph, b, k):
                n = updated[ph]
                if k == 0:
                    dve.wait_ge(ssq_done.sem, ssq_done.at(ph, b))
                else:
                    dve.wait_ge(newton.sem, newton.at(ph, b, k - 1))
                r = rinv_i[:, 0:n].bitcast(F32)
                if k == 0:
                    i = dve.tensor_scalar(var[:, 0:n], ssq[:, 0:n], 1.0 / D, EPS, ALU.mult, ALU.add)
                elif k == 1:
                    i = dve.tensor_scalar(seed[:, 0:n], var[:, 0:n].bitcast(I32), 1, None, ALU.logical_shift_right)
                elif k == 2:
                    i = dve.tensor_scalar(rinv_i[:, 0:n], seed[:, 0:n], -1.0, RSQRT_SEED, ALU.mult, ALU.add)
                elif k % 3 == 0:
                    i = dve.tensor_tensor(nt_a[:, 0:n], r, r, ALU.mult)
                elif k % 3 == 1:
                    i = dve.scalar_tensor_tensor(nt_b[:, 0:n], nt_a[:, 0:n], -0.5, var[:, 0:n], ALU.mult, ALU.mult)
                else:
                    i = dve.scalar_tensor_tensor(r, nt_b[:, 0:n], 1.5, r, ALU.add, ALU.mult)
                i.then_inc(newton.sem, 1)

            def scale(ph, b):
                n = updated[ph]
                dve.wait_ge(newton.sem, newton.at(ph, b, newton.per[ph] - 1))
                if (b - SLOTS).real:
                    dve.wait_ge(st_x.sem(b), st_x.at(ph, b - SLOTS))
                    if ph < 3:
                        dve.wait_ge(st_ends.sem(b), st_ends.at(ph, b - SLOTS))
                    if ph < 4:
                        dve.wait_ge(e_trans.sem, e_trans.at(ph, b - SLOTS))
                m = NG if ph == 3 else n
                i = dve.tensor_tensor(groups(xn[b.q], 0, m), groups(y[b.p], 0, m), spread(rinv, m), ALU.mult)
                if ph == 3:
                    i = dve.tensor_tensor(groups(xn[b.q], NG, EG)[:, 0:EG:2, :], groups(y[b.p], NG, TILES),
                                          rinv[:, NG:n].unsqueeze(2).broadcast_to([P, TILES, D]), ALU.mult)
                i.then_inc(ln_done.sem, 1)

            rinv = rinv_i[:, :].bitcast(F32)

            def body0(b):
                build_same(0, b)
                if (b - SLOTS).real:
                    dve.wait_ge(st_rows.sem(b), st_rows.at(0, b - SLOTS))
                    dve.wait_ge(dst_added, dst_at(0, b - SLOTS, 1))
                dve.tensor_copy(key_f[:, :], keyc[b.q][:, :]).then_inc(prep.sem, 1)
                dve.wait_ge(s_built.sem, s_built.at(0, b))
                dve.tensor_tensor(earlier[:, :, :], same[b.p][:, :, :], before[:, :].unsqueeze(1).broadcast_to([P, EG, P]),
                                  ALU.mult).then_inc(prep.sem, 1)
                dve.wait_ge(prep.sem, prep.at(0, b, 1))
                dve.tensor_reduce(dup[:, :], earlier[:, :, :], AX_X, ALU.add).then_inc(prep.sem, 1)
                dve.tensor_tensor(off[:, :], spare[:, :], key_f[:, :], ALU.subtract).then_inc(prep.sem, 1)
                dve.wait_ge(prep.sem, prep.at(0, b, 3))
                dve.tensor_scalar(dup1[:, :], dup[:, :], 1.0, None, ALU.min).then_inc(prep.sem, 1)
                dve.wait_ge(prep.sem, prep.at(0, b, 4))
                dve.tensor_tensor(off1[:, :], off[:, :], dup1[:, :], ALU.mult).then_inc(prep.sem, 1)
                dve.wait_ge(prep.sem, prep.at(0, b, 5))
                dve.tensor_tensor(row_f[:, :], off1[:, :], key_f[:, :], ALU.add).then_inc(prep.sem, 1)
                dve.wait_ge(prep.sem, prep.at(0, b, 6))
                dve.tensor_copy(s_rows[b.q][:, 0:EG], row_f[:, :]).then_inc(prep.sem, 1)
                dve.tensor_scalar(s_rows[b.q][:, EG:EG + TILES], row_f[:, 0:TILES], 2.0, 1.0, ALU.mult, ALU.add
                                  ).then_inc(prep.sem, 1)
                dve.tensor_scalar(s_rows[b.q][:, EG + TILES:2 * EG], row_f[:, TILES:EG], 2.0, None, ALU.mult
                                  ).then_inc(prep.sem, 1)

            steps(dve, body0, 0)

            def times_r(b, k):
                dve.wait_ge(gate_done.sem, gate_done.at(1, b, k))
                if (b - 2).real:
                    dve.wait_ge(tanh_done.sem, tanh_done.at(1, b - 2))
                c = buf(1, b, k)
                g = pG[:, 2 * c:2 * c + 2, :].rearrange("p a (g c) -> p (a g) c", c=256)
                dve.tensor_tensor(groups(pre_n[b.p], k * CH, CH), groups(gates[b.p], k * CH, CH, 2 * D)[:, :, 0:D],
                                  g[:, :, 3 * D:4 * D], ALU.mult).then_inc(rn_done.sem, 1)

            def plus_n(b, k):
                dve.wait_ge(rn_done.sem, rn_done.at(1, b, k))
                c = buf(1, b, k)
                g = pG[:, 2 * c:2 * c + 2, :].rearrange("p a (g c) -> p (a g) c", c=256)
                v = groups(pre_n[b.p], k * CH, CH)
                dve.tensor_tensor(v, v, g[:, :, 2 * D:3 * D], ALU.add).then_inc(g_used.sem, 1)

            def body1(s):
                f = s - 1
                if s.real:
                    times_r(s, 0)
                    times_r(s, 1)
                    plus_n(s, 0)
                    plus_n(s, 1)
                if f.real:
                    square_sums(1, f)
                    build_same(1, f)
                    newton_step(1, f, 0)
                if s.real:
                    times_r(s, 2)
                if f.real:
                    newton_step(1, f, 1)
                if s.real:
                    plus_n(s, 2)
                if f.real:
                    for k in range(2, 6):
                        newton_step(1, f, k)
                if s.real:
                    dve.wait_ge(tanh_done.sem, tanh_done.at(1, s))
                    dve.wait_ge(in_rows.sem(s), in_rows.at(1, s))
                    dve.tensor_tensor(groups(diff[s.p], 0, G), groups(act_n[s.p], 0, G), x_of(1, s, 0, G), ALU.subtract
                                      ).then_inc(diff_done.sem, 1)
                if f.real:
                    newton_step(1, f, 6)
                if s.real:
                    dve.wait_ge(diff_done.sem, diff_done.at(1, s))
                    dve.tensor_tensor(groups(diff[s.p], 0, G), groups(gates[s.p], 0, G, 2 * D)[:, :, D:2 * D],
                                      groups(diff[s.p], 0, G), ALU.mult).then_inc(zd_done.sem, 1)
                if f.real:
                    newton_step(1, f, 7)
                if s.real:
                    dve.wait_ge(zd_done.sem, zd_done.at(1, s))
                    dve.scalar_tensor_tensor(groups(y[s.p], 0, G), x_of(1, s, 0, G), 2.0, groups(diff[s.p], 0, G), ALU.mult, ALU.add
                                             ).then_inc(y_done.sem, 1)
                if f.real:
                    newton_step(1, f, 8)
                if s.real:
                    row_sums(1, s)
                if f.real:
                    newton_step(1, f, 9)
                    newton_step(1, f, 10)
                if s.real:
                    center(1, s)
                if f.real:
                    newton_step(1, f, 11)
                    scale(1, f)

            steps(dve, body1, 1)

            def add_first(b, k):
                dve.wait_ge(g_done.sem, g_done.at(2, b, k))
                sums = sums_of(2, b, k * CH, CH)
                dve.tensor_tensor(groups(diff[b.p], k * CH, CH), groups(pG[:, buf(2, b, k), :], 0, CH), sums[:, :, 0:D],
                                  ALU.add).then_inc(g_used.sem, 1)

            def body2(s):
                f = s - 1
                if f.real:
                    square_sums(2, f)
                if s.real:
                    add_first(s, 0)
                    add_first(s, 1)
                if f.real:
                    build_same(2, f)
                if s.real:
                    dve.wait_ge(gathered.sem(s), gathered.at(2, s))
                    add_first(s, 2)
                if f.real:
                    dve.wait_ge(std_done.sem, std_done.at(2, f))
                    dve.reciprocal(rinv, std[:, :]).then_inc(newton.sem, 1)
                if s.real:
                    dve.wait_ge(g_used.sem, g_used.at(2, s, 2))
                    dve.tensor_tensor(groups(y[s.p], 0, G), groups(diff[s.p], 0, G),
                                      sums_of(2, s, 0, G)[:, :, D:2 * D], ALU.add).then_inc(y_done.sem, 1)
                if f.real:
                    scale(2, f)
                if s.real:
                    row_sums(2, s)
                    center(2, s)

            steps(dve, body2, 1)

            def means(b):
                n = updated[3]
                dve.wait_ge(in_rows.sem(b), in_rows.at(3, b))
                dve.wait_ge(gathered.sem(b), gathered.at(3, b))
                sums = sums_of(3, b, 0, n)
                dve.tensor_scalar(cnt[:, 0:n].unsqueeze(2), sums[:, :, D:D + 1], 1.0, None, ALU.max).then_inc(cnt_done.sem, 1)
                dve.wait_ge(cnt_done.sem, cnt_done.at(3, b, 0))
                dve.reciprocal(rcnt[:, 0:n], cnt[:, 0:n]).then_inc(cnt_done.sem, 1)
                dve.wait_ge(cnt_done.sem, cnt_done.at(3, b, 1))
                dve.tensor_tensor(groups(rows[b.q], 0, n, 2 * D)[:, :, D:2 * D], sums[:, :, 0:D], spread(rcnt, n), ALU.mult
                                  ).then_inc(pre_done.sem, 1)

            def relu_plus_x(b, k):
                dve.wait_ge(g_done.sem, g_done.at(3, b, k))
                n = min(updated[3], (k + 1) * CH) - k * CH
                dve.scalar_tensor_tensor(groups(y[b.p], k * CH, n), groups(pG[:, buf(3, b, k), :], 0, n), 0.0,
                                         x_of(3, b, k * CH, n), ALU.max, ALU.add).then_inc(y_done.sem, 1)

            def body3(s):
                f = s - 1
                if s.reg is None and s.c == 0:
                    means(s)
                if (s + 1).real:
                    means(s + 1)
                if f.real:
                    square_sums(3, f)
                    build_same(3, f)
                    for k in range(0, 4):
                        newton_step(3, f, k)
                for k in range(3):
                    if s.real:
                        relu_plus_x(s, k)
                    if f.real:
                        newton_step(3, f, 4 + k)
                if f.real:
                    newton_step(3, f, 7)
                if s.real:
                    row_sums(3, s)
                if f.real:
                    newton_step(3, f, 8)
                    newton_step(3, f, 9)
                if s.real:
                    center(3, s)
                if f.real:
                    newton_step(3, f, 10)
                    newton_step(3, f, 11)
                    scale(3, f)

            steps(dve, body3, 1, ahead=2)

            def eps_x_plus_sums(b):
                dve.wait_ge(in_rows.sem(b), in_rows.at(4, b))
                r = rows[b.q]
                dve.scalar_tensor_tensor(r[:, W:W + NG * D], r[:, 0:NG * D], eps1p[:, 0:1],
                                         r[:, RAW:RAW + NG * D], ALU.mult, ALU.add).then_inc(pre_done.sem, 1)

            def body4(s):
                f = s - 1
                if s.reg is None and s.c == 0:
                    eps_x_plus_sums(s)
                if (s + 1).real:
                    eps_x_plus_sums(s + 1)
                if f.real:
                    square_sums(4, f)
                    for k in range(0, 8):
                        newton_step(4, f, k)
                if s.real:
                    dve.wait_ge(g_used.sem, g_used.at(4, s, 1))
                    dve.tensor_tensor(y[s.p][:, 0:NG * D], act_n[s.p][:, 0:NG * D], rows[s.q][:, 0:NG * D], ALU.add
                                      ).then_inc(y_done.sem, 1)
                if f.real:
                    newton_step(4, f, 8)
                if s.real:
                    row_sums(4, s)
                if f.real:
                    newton_step(4, f, 9)
                    newton_step(4, f, 10)
                if s.real:
                    center(4, s)
                if f.real:
                    newton_step(4, f, 11)
                    scale(4, f)

            steps(dve, body4, 1, ahead=2)


def kernel(**inputs):
    import numpy as np
    import concourse.bacc as bacc
    from concourse.bass_utils import run_bass_kernel_spmd

    a = {k: np.asarray(v) for k, v in inputs.items()}
    slots = PAIRS * TILES

    def by_tile(v, pad):
        full = np.full((P * slots,) + v.shape[1:], pad, v.dtype)
        full[:E] = v
        return full.reshape((P, PAIRS, TILES) + v.shape[1:])

    def both(pad):
        ends = np.stack([by_tile(a["src"], pad), by_tile(a["dst"], pad)], axis=2)
        return np.ascontiguousarray(ends.transpose(1, 0, 2, 3).reshape(PAIRS, P, EG))

    arrays = {
        "x": a["x"],
        "gather_rows": both(0),
        "key_cols": both(N),
        "key_rows": np.ascontiguousarray(both(N).transpose(0, 2, 1).reshape(PAIRS, EG * P)),
        "attr_rows": np.ascontiguousarray(
            by_tile(a["edge_weight1"][:, 0], 0).transpose(1, 2, 0).reshape(PAIRS, TILES * P)),
        "attr64": by_tile(a["edge_attr_64"], 0).reshape(P, PAIRS, TILES * D),
    }
    turned = ("L0_gnn_W1", "L0_gnn_W2", "L0_gnn_W_ih", "L0_gnn_W_hh", "L1_gnn_w0_w", "L1_gnn_w1_w")
    for k, v in a.items():
        if k.startswith("L"):
            arrays[k.replace("_gnn", "")] = np.ascontiguousarray(v.T) if k in turned else v

    nc = bacc.Bacc("TRN2", target_bir_lowering=False, num_devices=1)
    t = {k: nc.dram_tensor(k, v.shape, mybir.dt.from_np(v.dtype), kind="ExternalInput").ap() for k, v in arrays.items()}
    out = nc.dram_tensor("new_x", (N, D), F32, kind="ExternalOutput").ap()
    build(nc, t["x"], t["gather_rows"], t["key_cols"], t["key_rows"], t["attr_rows"], t["attr64"], t, out)
    r = run_bass_kernel_spmd(nc, [arrays], core_ids=[0])
    return r.results[0]["new_x"]
```

```python
from contextlib import ExitStack

import concourse.bass as bass
from concourse import mybir

F32 = mybir.dt.float32
BF16 = mybir.dt.bfloat16
I32 = mybir.dt.int32
ALU = mybir.AluOpType
ACT = mybir.ActivationFunctionType
AX_X = mybir.AxisListType.X

P = 128
N, D, E = 100000, 64, 25000
NODES = 1024
NG = NODES // P
TILES = 2
EG = 2 * TILES
G = NG + EG
PAIRS = -(-N // NODES)
ROWS = PAIRS * NODES
assert PAIRS * TILES * P >= E and ROWS - N > P
W = G * D
RAW = 2 * W
CH = 4
EPS = 1e-5
RSQRT_SEED = float(0x5F3759DF)
PHASES = 5
CHUNKS = {1: 3, 2: 3, 3: 3, 4: 2}
LAST_ROWS = N - (PAIRS - 1) * NODES
LAST_P = LAST_ROWS // NG
assert LAST_P * NG == LAST_ROWS
NEWTON = 12
SLOTS = 4
BATCHED = (1, 3)
NORM_SKEW = {1: 5, 2: 3, 3: 5}
KEYS_SKEW = {1: 4, 2: 2, 3: 5}
SIDX_SKEW = {1: 7, 2: 5, 3: 7}
SCATTER_SKEW = {0: 3, 1: 8, 2: 7, 3: 10}
STORE_SKEW = {1: 8, 2: 6, 3: 8, 4: 6}
WEIGHT_DMAS = 17
BIAS_DMAS = 10
ZERO_FIRST = 12


class Pair:

    def __init__(self, c, reg=None):
        self.c, self.reg = c, reg
        self.p = c % 2
        self.q = c % SLOTS

    def __sub__(self, k):
        return Pair(self.c - k, self.reg)

    def __add__(self, k):
        return Pair(self.c + k, self.reg)

    def times(self, m, add):
        n = m * self.c + add
        return n if self.reg is None else self.reg * (SLOTS * m) + n

    def rounds(self, m, add):
        n = m * (self.c // SLOTS) + add
        return n if self.reg is None else self.reg * m + n

    @property
    def real(self):
        return self.reg is not None or 0 <= self.c < PAIRS

    @property
    def index(self):
        return self.c if self.reg is None else self.reg * SLOTS + self.c


def steps(eng, body, skew, ahead=0):
    total = PAIRS + skew
    lead = -(-(skew + SLOTS) // SLOTS) * SLOTS
    tail = skew + max(1, ahead)
    tail += (total - lead - tail) % SLOTS
    for s in range(lead):
        body(Pair(s))
    with eng.Fori(0, (total - lead - tail) // SLOTS) as i:
        for k in range(SLOTS):
            body(Pair(lead + k, i))
    for s in range(total - tail, total):
        body(Pair(s))


def first(s):
    return s.reg is None and s.c == 0


class Event:

    def __init__(self, sem, per):
        self.sem, self.per = sem, per

    def end(self, ph):
        return sum(PAIRS * n for q, n in self.per.items() if q < ph)

    def at(self, ph, b, k=0):
        return b.times(self.per[ph], self.end(ph) + k + 1)


class Landed:

    def __init__(self, sems, per):
        self.sems, self.per = sems, per

    def sem(self, b):
        return self.sems[b.q]

    def end(self, ph, q):
        return sum(16 * n * len(range(q, PAIRS, SLOTS)) for f, n in self.per.items() if f < ph)

    def at(self, ph, b):
        n = 16 * self.per[ph]
        return b.rounds(n, self.end(ph, b.q) + n)


def build(nc, x_in, gather_rows, key_cols, key_rows, attr_rows, attr64, weights, out):
    w = weights
    dram = lambda name, shape, dt: nc.dram_tensor(name, shape, dt, kind="Internal").ap()
    x_dram = dram("x_nodes", [ROWS, D], F32)
    ends_dram = dram("x_edge_ends", [PAIRS, P, EG * D], F32)
    rows_dram = dram("scatter_rows", [PAIRS, P, 2 * EG], I32)
    table = [dram("sums0", [ROWS, D], F32), dram("sums1", [ROWS, 2 * D], F32),
             dram("sums2", [ROWS, D + 1], F32), dram("sums3", [ROWS, D], F32)]
    width = [D, 2 * D, D + 1, D]
    halves1 = table[1].rearrange("n (h d) -> (n h) d", h=2)

    def nodes_of(t):
        return t.rearrange("(b p r) d -> b p (r d)", p=P, r=NG)

    with ExitStack() as ctx:
        def sb(name, shape, dt=F32):
            return ctx.enter_context(nc.sbuf_tensor(name, shape, dt))

        def ps(name, shape):
            return ctx.enter_context(nc.psum_tensor(name, shape, F32))

        def sem(name):
            return ctx.enter_context(nc.semaphore(name))

        def event(name, per):
            return Event(sem(name), per)

        def landed(name, per):
            return Landed([sem(f"{name}_{q}") for q in range(SLOTS)], per)

        ident = sb("ident", [P, P])
        before = sb("before", [P, P])
        spare = sb("spare", [P, EG])
        spare_i = sb("spare_i", [P, EG], I32)
        zeros = sb("zeros", [P, 2 * NG * D])
        w_gru = sb("w_gru", [P, 4 * D])
        w_h = sb("w_h", [P, 2 * D])
        w_e = sb("w_e", [1, 2 * D])
        b_h = sb("b_h", [P, 1])
        w_m0 = sb("w_m0", [P, D])
        w_self = sb("w_self", [P, 2 * D])
        w_nb = sb("w_nb", [P, 2 * D])
        w_m2 = sb("w_m2", [P, D])
        w_u2 = sb("w_u2", [P, D])
        w_m3 = sb("w_m3", [P, D])
        w_u3 = sb("w_u3", [P, 2 * D])
        eps_col = sb("eps_col", [P, 1])
        eps1 = sb("eps1", [P, 1])
        eps1p = sb("eps1p", [P, 1])
        BIAS = {"gru": (0, 512), "m0": (512, 128), "self": (640, 256), "nb": (896, 256), "m2": (1152, 128),
                "u2": (1280, 256), "m3": (1536, 128), "u3": (1664, 256)}
        NB = 1920
        ONCE = {name: (0, 256) if name == "gru" else (192 + D * i, D) for i, name in enumerate(BIAS)}
        NO = 192 + D * len(BIAS)
        bias = sb("bias", [65, NO])
        bias_hh = sb("bias_hh", [65, 256])
        bias_hi = sb("bias_hi", [65, NO], BF16)
        bias_mid = sb("bias_mid", [65, NO], BF16)
        bias_lo = sb("bias_lo", [65, NO], BF16)
        bias_r1 = sb("bias_r1", [65, NO])
        bias_r2 = sb("bias_r2", [65, NO])
        bias3 = sb("bias3", [65, NB], BF16)
        ones65 = sb("ones65", [65, P], BF16)

        two = range(2)
        rows = [sb(f"rows{p}", [P, 4 * W]) for p in range(SLOTS)]
        g_rows = [sb(f"g_rows{p}", [P, EG], I32) for p in range(SLOTS)]
        s_rows = [sb(f"s_rows{p}", [P, 2 * EG], I32) for p in range(SLOTS)]
        keyc = [sb(f"keyc{p}", [P, EG], I32) for p in range(SLOTS)]
        keyr = [sb(f"keyr{p}", [P, EG * P], I32) for p in range(SLOTS)]
        attr_r = [sb(f"attr_r{p}", [1, TILES * P]) for p in range(SLOTS)]
        xt = [sb(f"xt{p}", [P, CH * P]) for p in two]
        gates = [sb(f"gates{p}", [P, G * 2 * D]) for p in two]
        pre_n = [sb(f"pre_n{p}", [P, W]) for p in two]
        act_n = [sb(f"act_n{p}", [P, W]) for p in two]
        diff = [sb(f"diff{p}", [P, W]) for p in two]
        y = [sb(f"y{p}", [P, W]) for p in range(SLOTS)]
        sq = [sb(f"sq{p}", [P, W]) for p in two]
        xn = [sb(f"xn{p}", [P, W]) for p in range(SLOTS)]
        same = [sb(f"same{p}", [P, EG, P]) for p in two]
        earlier = sb("earlier", [P, EG, P])
        et = [sb(f"et{p}", [P, TILES * P]) for p in two]
        hid = [sb(f"hid{p}", [P, TILES * P]) for p in two]
        msg = [sb(f"msg{p}", [P, 4 * D + 2]) for p in two]
        summed = [sb(f"summed{p}", [P, EG * (D + 1)]) for p in range(SLOTS)]
        tot = sb("tot", [P, G])
        ssq = sb("ssq", [P, 2, G])
        var = sb("var", [P, 2, G])
        seed = sb("seed", [P, 2, G], I32)
        rinv_i = [sb(f"rinv_i{p}", [P, 2, G], I32) for p in two]
        nt_a = sb("nt_a", [P, 2, G])
        nt_b = sb("nt_b", [P, 2, G])
        std = sb("std", [P, G])
        cnt = sb("cnt", [P, G])
        rcnt = sb("rcnt", [P, G])
        key_f = sb("key_f", [P, EG])
        dup = sb("dup", [P, EG])
        dup1 = sb("dup1", [P, EG])
        off = sb("off", [P, EG])
        off1 = sb("off1", [P, EG])
        row_f = sb("row_f", [P, EG])

        pT = ps("pT", [P, 2, 512])
        pG = ps("pG", [P, 4, 512])
        pEM = ps("pEM", [P, 512])
        pE, pM = pEM[:, 0:256], pEM[:, 256:512]
        pD = ps("pD", [P, 512])

        w_landed = sem("w_landed")
        b_landed = sem("b_landed")
        zero0 = sem("zero0")
        zeroed = landed("zeroed", {0: 1, 1: 1, 2: 1})
        in_rows = landed("in_rows", {1: 3, 2: 3, 3: 3, 4: 2})
        in_gidx = landed("in_gidx", {0: 1, 1: 1, 2: 1, 3: 1})
        in_keys = landed("in_keys", {0: 3, 1: 2, 2: 2, 3: 2})
        in_sidx = landed("in_sidx", {1: 1, 2: 1, 3: 1})
        in_attr = landed("in_attr", {3: 1})
        gathered = landed("gathered", {0: 4, 1: 4, 2: 4, 3: 2})
        st_x = landed("st_x", {1: 1, 2: 1, 3: 1, 4: 1})
        st_ends = landed("st_ends", {0: 1, 1: 1, 2: 1})
        st_rows = landed("st_rows", {0: 1})
        dst_added = sem("dst_added")
        src_added = sem("src_added")

        ready = sem("ready")
        pool_ready = sem("pool_ready")
        held = [sem("held_sp"), sem("held_pool")]
        prep_w = sem("prep_w")
        e03 = {0: 1, 1: 1, 2: 1, 3: 1}
        u14 = {1: 1, 2: 1, 3: 1, 4: 1}
        t_done = event("t_done", CHUNKS)
        t_copied = event("t_copied", CHUNKS)
        g_done = event("g_done", CHUNKS)
        g_used = event("g_used", {1: 3, 2: 3, 4: 2})
        gate_done = event("gate_done", {1: 3})
        rn_done = event("rn_done", {1: 3})
        tanh_done = event("tanh_done", {1: 1})
        diff_done = event("diff_done", {1: 1})
        zd_done = event("zd_done", {1: 1})
        cnt_done = event("cnt_done", {3: 2})
        pre_done = event("pre_done", {3: 1, 4: 1})
        y_done = event("y_done", {1: 1, 2: 1, 3: 3, 4: 1})
        sum_done = event("sum_done", u14)
        cen_done = event("cen_done", u14)
        sq_done = event("sq_done", u14)
        ssq_done = event("ssq_done", u14)
        std_done = event("std_done", {2: 1})
        newton = event("newton", {1: NEWTON // 2, 2: 1, 3: NEWTON // 2, 4: NEWTON})
        ln_done = event("ln_done", u14)
        e_trans = event("e_trans", e03)
        e_copied = event("e_copied", e03)
        h_mm = event("h_mm", {0: 1})
        h_act = event("h_act", {0: 1})
        m_mm = event("m_mm", e03)
        m_act = event("m_act", e03)
        s_built = event("s_built", e03)
        prep = event("prep", {0: 10})
        d_mm = event("d_mm", e03)
        d_act = event("d_act", e03)

        def hold(eng):
            eng.sem_inc(held[eng is nc.gpsimd], 1)

        def dst_at(ph, b, t):
            return b.times(32, 32 * PAIRS * ph + 16 * (t + 1))

        def src_at(b, t):
            return b.times(32, 16 * (t + 1))

        def bias_of(name, n=None):
            a, m = BIAS[name]
            return bias3[:, a:a + (n or m)]

        def buf(ph, b, k):
            return (CHUNKS[ph] * b.p + k) % 2

        def bank(ph, b, k):
            return 2 * buf(1, b, k) if ph == 1 else (CHUNKS[ph] * b.q + k) % 4

        def groups(t, a, n, c=D):
            return t[:, a * c:(a + n) * c].rearrange("p (g c) -> p g c", c=c)

        def spread(t, n, c=D):
            return t[:, 0:n].unsqueeze(2).broadcast_to([P, n, c])

        def x_of(ph, b, a, n):
            if ph in (1, 3):
                return groups(rows[b.q], a, n, 2 * D)[:, :, 0:D]
            return groups(rows[b.q], a, n)

        def sums_of(ph, b, a, n):
            if ph == 1:
                return groups(rows[b.q], a, n, 2 * D)[:, :, D:2 * D]
            return groups(rows[b.q][:, RAW:4 * W], a, n, width[ph - 1])

        updated = {1: G, 2: G, 3: NG + TILES, 4: NG}

        def may_scale(eng, ph, b):
            last = NEWTON - 1 if ph in BATCHED and b.p == 0 else newton.per[ph] - 1
            eng.wait_ge(newton.sem, newton.at(ph, b, last))
            if (b - SLOTS).real:
                eng.wait_ge(st_x.sem(b), st_x.at(ph, b - SLOTS))
                if ph < 3:
                    eng.wait_ge(st_ends.sem(b), st_ends.at(ph, b - SLOTS))
                if ph < 4:
                    eng.wait_ge(e_trans.sem, e_trans.at(ph, b - SLOTS))

        block = ctx.enter_context(nc.Block())

        @block.sync
        def _(sp):
            def put(dst, src):
                sp.dma_start(dst, src).then_inc(w_landed, 16)

            sp.wait_ge(ready, 2)
            put(w_gru[0:D, 0:2 * D], w["L0_W_hh"][:, 0:2 * D])
            put(w_gru[0:D, 3 * D:4 * D], w["L0_W_hh"][:, 2 * D:3 * D])
            put(w_gru[D:P, 0:3 * D], w["L0_W_ih"])
            put(w_h[:, :], w["L0_W1"][0:P, :])
            put(w_e[:, :], w["L0_W1"][P:P + 1, :])
            put(b_h[:, :], w["L0_b1"].rearrange("(p o) -> p o", o=1))
            put(w_m0[:, :], w["L0_W2"])
            for dst, name in ((w_self, "L1_w0_w"), (w_nb, "L1_w1_w"), (w_u3, "L3_W_upd")):
                put(dst[0:D, 0:D], w[name])
                put(dst[D:P, D:P], w[name])
            put(w_m2[:, :], w["L2_W_msg"])
            put(w_u2[:, :], w["L2_W_upd"])
            put(w_m3[:, :], w["L3_W_msg"])
            put(eps1[:, :], w["L3_eps"].unsqueeze(0).broadcast_to([P, 1]))

            def load_gidx(ph, b):
                if (b - SLOTS).real:
                    sp.wait_ge(gathered.sem(b), gathered.at(ph, b - SLOTS))
                hold(sp)
                sp.dma_start(g_rows[b.q][:, :], gather_rows[b.index]).then_inc(in_gidx.sem(b), 16)

            def next_gidx(ph, s):
                if first(s) and ph == 0:
                    load_gidx(ph, s)
                if (s + 1).real:
                    load_gidx(ph, s + 1)

            def load_keys(ph, b):
                if (b - SLOTS).real:
                    sp.wait_ge(s_built.sem, s_built.at(ph, b - SLOTS))
                    if ph == 0:
                        hold(sp)
                        sp.wait_ge(prep.sem, prep.at(0, b - SLOTS, 0))
                        hold(sp)
                        sp.wait_ge(h_mm.sem, h_mm.at(0, b - SLOTS))
                hold(sp)
                skip = 0 if ph < 2 else TILES
                sp.dma_start(keyr[b.q][:, skip * P:EG * P],
                             key_rows[b.index][skip * P:EG * P].unsqueeze(0).broadcast_to([P, (EG - skip) * P])
                             ).then_inc(in_keys.sem(b), 16)
                sp.dma_start(keyc[b.q][:, :], key_cols[b.index]).then_inc(in_keys.sem(b), 16)
                if ph == 0:
                    sp.dma_start(attr_r[b.q][:, :], attr_rows[b.index].unsqueeze(0)).then_inc(in_keys.sem(b), 16)

            def zero(ph, b):
                n = NG * width[ph + 1]
                sp.dma_start(nodes_of(table[ph + 1])[b.index], zeros[:, 0:n]).then_inc(zeroed.sem(b), 16)

            def load_rows(ph, b, last=False):
                if (b - SLOTS).real:
                    sp.wait_ge(y_done.sem, y_done.at(ph, b - SLOTS, y_done.per[ph] - 1))
                hold(sp)
                if ph > 1:
                    x, to = x_dram, x_of(ph, b, 0, NG)
                    src = x[:, :].rearrange("(b p r) d -> b p r d", p=P, r=NG)[b.index]
                elif last:
                    to = x_of(1, b, 0, NG)[0:LAST_P]
                    src = x_in[(PAIRS - 1) * NODES:N, :].rearrange("(p r) d -> p r d", r=NG)
                else:
                    to = x_of(1, b, 0, NG)
                    src = x_in[0:(PAIRS - 1) * NODES, :].rearrange("(b p r) d -> b p r d", p=P, r=NG)[b.index]
                sp.dma_start(to, src).then_inc(in_rows.sem(b), 16)
                sp.dma_start(sums_of(ph, b, 0, NG),
                             table[ph - 1].rearrange("(b p r) d -> b p r d", p=P, r=NG)[b.index]
                             ).then_inc(in_rows.sem(b), 16)
                if ph < 4:
                    m = updated[ph] - NG
                    ends = ends_dram[b.index].rearrange("p (g c) -> p g c", c=D)
                    sp.dma_start(x_of(ph, b, NG, m), ends if ph < 3 else ends[:, 0:EG:2, :]
                                 ).then_inc(in_rows.sem(b), 16)

            def load_sidx(ph, b):
                if (b - SLOTS).real:
                    sp.wait_ge(dst_added, dst_at(ph, b - SLOTS, 1))
                    if ph == 1:
                        hold(sp)
                        sp.wait_ge(src_added, src_at(b - SLOTS, 1))
                hold(sp)
                sp.dma_start(s_rows[b.q][:, :], rows_dram[b.index]).then_inc(in_sidx.sem(b), 16)

            def load_attr(b):
                if (b - SLOTS).real:
                    sp.wait_ge(e_trans.sem, e_trans.at(3, b - SLOTS))
                hold(sp)
                sp.dma_start(groups(xn[b.q], NG, EG)[:, 1:EG:2, :],
                             attr64[:, b.index, :].rearrange("p (t c) -> p t c", c=D)).then_inc(in_attr.sem(b), 16)

            def store(ph, b, last=False):
                sp.wait_ge(ln_done.sem, ln_done.at(ph, b))
                hold(sp)
                v = xn[b.q]
                if ph < 4:
                    sp.dma_start(nodes_of(x_dram)[b.index], v[:, 0:NG * D]).then_inc(st_x.sem(b), 16)
                elif last:
                    sp.dma_start(out[(PAIRS - 1) * NODES:N, :].rearrange("(p r) d -> p (r d)", r=NG),
                                 v[0:LAST_P, 0:NG * D]).then_inc(st_x.sem(b), 16)
                else:
                    sp.dma_start(nodes_of(out[0:(PAIRS - 1) * NODES, :])[b.index], v[:, 0:NG * D]
                                 ).then_inc(st_x.sem(b), 16)
                if ph < 3:
                    sp.dma_start(ends_dram[b.index], v[:, NG * D:G * D]).then_inc(st_ends.sem(b), 16)

            def body0(s):
                next_gidx(0, s)
                if s.real:
                    load_keys(0, s)
                    zero(0, s)
                b = s - 1
                if b.real:
                    sp.wait_ge(gathered.sem(b), gathered.at(0, b))
                    hold(sp)
                    sp.dma_start(ends_dram[b.index], rows[b.q][:, NG * D:G * D]).then_inc(st_ends.sem(b), 16)
                b = s - 3
                if b.real:
                    sp.wait_ge(prep.sem, prep.at(0, b, 9))
                    hold(sp)
                    sp.dma_start(rows_dram[b.index], s_rows[b.q][:, :]).then_inc(st_rows.sem(b), 16)

            steps(sp, body0, 3, ahead=2)

            for ph in range(1, PHASES):
                if ph < 4:
                    sp.wait_ge(gathered.sems[0], gathered.end(ph, 0))
                    load_gidx(ph, Pair(0))
                sp.wait_ge(dst_added, 32 * PAIRS * ph)
                if ph == 2:
                    sp.wait_ge(src_added, 32 * PAIRS)
                for q in range(SLOTS):
                    sp.wait_ge(st_ends.sems[q], st_ends.end(ph, q))
                    if ph == 1:
                        sp.wait_ge(st_rows.sems[q], st_rows.end(ph, q))
                    if ph > 1:
                        sp.wait_ge(st_x.sems[q], st_x.end(ph, q))
                    if ph < 4:
                        sp.wait_ge(zeroed.sems[q], zeroed.end(ph, q))

                def body(s, ph=ph):
                    last = s.reg is None and s.c == PAIRS - 1
                    if ph < 4:
                        next_gidx(ph, s)
                    if s.real:
                        load_rows(ph, s, last)
                    if ph < 4 and (s - KEYS_SKEW[ph]).real:
                        load_keys(ph, s - KEYS_SKEW[ph])
                        if ph == 3:
                            load_attr(s - KEYS_SKEW[ph])
                    if ph < 4 and (s - SIDX_SKEW[ph]).real:
                        load_sidx(ph, s - SIDX_SKEW[ph])
                    b = s - STORE_SKEW[ph]
                    if b.real:
                        store(ph, b, b.reg is None and b.c == PAIRS - 1)
                        if ph < 3:
                            zero(ph, b)

                steps(sp, body, STORE_SKEW[ph], ahead=2)
            for q in range(SLOTS):
                sp.wait_ge(st_x.sems[q], st_x.end(PHASES, q))

        @block.gpsimd
        def _(pool):
            pool.memset(ident[:, :], 0.0).then_inc(pool_ready, 1)
            pool.memset(before[:, :], 1.0).then_inc(pool_ready, 1)
            pool.wait_ge(pool_ready, 2)
            pool.affine_select(out=ident[:, :], in_=ident[:, :], compare_op=ALU.not_equal, fill=1.0, base=0,
                               pattern=[[-1, P]], channel_multiplier=1).then_inc(pool_ready, 1)
            pool.affine_select(out=before[:, :], in_=before[:, :], compare_op=ALU.is_gt, fill=0.0, base=0,
                               pattern=[[-1, P]], channel_multiplier=1).then_inc(pool_ready, 1)
            pool.iota(spare_i[:, :], pattern=[[0, EG]], base=N + 1, channel_multiplier=1).then_inc(pool_ready, 1)

            def gather(ph, b, j):
                src = x_in if ph == 0 else table[ph - 1]
                to = x_of(0, b, NG + j, 1) if ph == 0 else sums_of(ph, b, NG + j, 1)
                col = j if ph == 3 else (j % 2) * TILES + j // 2
                pool.indirect_dma_start(to[:, 0, :], None, src,
                                        bass.IndirectOffsetOnAxis(g_rows[b.q][:, col:col + 1], 0)
                                        ).then_inc(gathered.sem(b), 16)

            def may_gather(ph, b):
                pool.wait_ge(in_gidx.sem(b), in_gidx.at(ph, b))
                if not (b - SLOTS).real:
                    return
                if ph == 0:
                    pool.wait_ge(e_trans.sem, e_trans.at(0, b - SLOTS))
                    pool.wait_ge(st_ends.sem(b), st_ends.at(0, b - SLOTS))
                elif ph == 1:
                    pool.wait_ge(t_done.sem, t_done.at(1, b - SLOTS, 2))
                elif ph == 2:
                    pool.wait_ge(y_done.sem, y_done.at(2, b - SLOTS))
                else:
                    pool.wait_ge(pre_done.sem, pre_done.at(3, b - SLOTS))

            def scatter(ph, b, t):
                if t == 0:
                    pool.wait_ge(d_act.sem, d_act.at(ph, b))
                    if ph:
                        pool.wait_ge(in_sidx.sem(b), in_sidx.at(ph, b))
                    else:
                        pool.wait_ge(prep.sem, prep.at(0, b, 9))
                        if first(b):
                            pool.wait_ge(zero0, 32)
                if not (first(b) and t == 0):
                    pool.wait_ge(dst_added, dst_at(ph, b, t - 1))
                n = D + 1 if ph == 2 else D
                dst = halves1 if ph == 1 else table[ph]
                hold(pool)
                col = TILES + t + (EG if ph == 1 else 0)
                at = (TILES + t) * D if ph == 1 else t * n
                pool.indirect_dma_start(dst, bass.IndirectOffsetOnAxis(s_rows[b.q][:, col:col + 1], 0),
                                        summed[b.q][:, at:at + n], None, compute_op=ALU.add).then_inc(dst_added, 16)
                if ph == 1:
                    if not (first(b) and t == 0):
                        pool.wait_ge(src_added, src_at(b, t - 1))
                    hold(pool)
                    col = t + EG
                    pool.indirect_dma_start(dst, bass.IndirectOffsetOnAxis(s_rows[b.q][:, col:col + 1], 0),
                                            summed[b.q][:, t * D:(t + 1) * D], None, compute_op=ALU.add
                                            ).then_inc(src_added, 16)

            for ph in range(4):
                if ph > 0:
                    for q in range(SLOTS):
                        pool.wait_ge(zeroed.sems[q], zeroed.end(ph, q))
                    pool.wait_ge(dst_added, 32 * PAIRS * ph)
                    if ph == 2:
                        pool.wait_ge(src_added, 32 * PAIRS)
                skew = SCATTER_SKEW[ph]

                def body(s, ph=ph, skew=skew):
                    b = s - skew
                    m = TILES if ph == 3 else EG
                    if s.real:
                        may_gather(ph, s)
                    for t in range(TILES):
                        if b.real:
                            scatter(ph, b, t)
                        if s.real:
                            for j in range(t * m // 2, (t + 1) * m // 2):
                                gather(ph, s, j)

                steps(pool, body, skew)
            pool.wait_ge(dst_added, 32 * PAIRS * 4)

            def gelu_plus_x(b):
                pool.wait_ge(g_used.sem, g_used.at(4, b, 1))
                pool.wait_ge(in_rows.sem(b), in_rows.at(4, b))
                if (b - SLOTS).real:
                    pool.wait_ge(ln_done.sem, ln_done.at(4, b - SLOTS))
                pool.tensor_tensor(y[b.q][:, 0:NG * D], act_n[b.p][:, 0:NG * D], rows[b.q][:, 0:NG * D], ALU.add
                                   ).then_inc(y_done.sem, 1)

            steps(pool, gelu_plus_x, 0)

        @block.tensor
        def _(pe):
            pe.wait_ge(pool_ready, 5)
            pe.wait_ge(ready, 3)

            def transpose_chunk(ph, b, k):
                last = min(updated[ph], (k + 1) * CH)
                if k == 0:
                    pe.wait_ge(in_rows.sem(b), in_rows.at(ph, b))
                    if ph > 2:
                        pe.wait_ge(pre_done.sem, pre_done.at(ph, b))
                if k == 2 and ph == 1:
                    pe.wait_ge(gathered.sem(b), gathered.at(ph, b))
                c = buf(ph, b, k)
                if b.reg is not None or CHUNKS[ph] * b.c + k >= 2:
                    pe.wait_ge(t_copied.sem, t_copied.at(ph, b, k - 2))
                per = 1 if ph in (1, 3) else 2
                a = W if ph == 4 else 0
                for i, g in enumerate(range(k * CH, last, per)):
                    at = a + g * P // per
                    t = pe.transpose(pT[:, c, i * P:(i + 1) * P], rows[b.q][:, at:at + P], ident[:, :])
                t.then_inc(t_done.sem, 1)

            def update_chunk(ph, b, k):
                pe.wait_ge(t_copied.sem, t_copied.at(ph, b, k))
                c, g0 = buf(ph, b, k), bank(ph, b, k)
                ring = 2 if ph == 1 else 4
                if b.reg is not None or CHUNKS[ph] * b.c + k >= ring:
                    used = y_done if ph == 3 else g_used
                    pe.wait_ge(used.sem, used.at(ph, b, k - ring))
                n = min(updated[ph], (k + 1) * CH) - k * CH
                x = xt[c]
                if ph == 1:
                    for g in range(n):
                        o = pG[:, g0 + g // 2, (g % 2) * 256:(g % 2 + 1) * 256]
                        if g % 2 == 0:
                            pe.matmul(pG[:, g0 + g // 2, :], ones65[:, :], bias_of("gru"), start=True, stop=False)
                        m = pe.matmul(o, x[:, g * P:(g + 1) * P], w_gru[:, :], start=False, stop=(g % 2 == 1))
                else:
                    name = {2: "self", 3: "u2", 4: "u3"}[ph]
                    wt = {2: w_self, 3: w_u2, 4: w_u3}[ph]
                    per = D if ph == 3 else 2 * D
                    pe.matmul(pG[:, g0, 0:n * D], ones65[:, :], bias_of(name, n * D), start=True, stop=False)
                    for i in range(n * D // per):
                        m = pe.matmul(pG[:, g0, i * per:(i + 1) * per], x[:, i * P:(i + 1) * P], wt[:, :],
                                      start=False, stop=(i == n * D // per - 1))
                m.then_inc(g_done.sem, 1)

            def edge_transpose(ph, b):
                if ph == 0:
                    pe.wait_ge(gathered.sem(b), gathered.at(0, b))
                    src = rows[b.q]
                else:
                    pe.wait_ge(ln_done.sem, ln_done.at(ph, b))
                    src = xn[b.q]
                if ph == 3:
                    pe.wait_ge(in_attr.sem(b), in_attr.at(3, b))
                if (b - 1).real:
                    last = h_act if ph == 0 else m_act
                    pe.wait_ge(last.sem, last.at(ph, b - 1))
                for t in range(TILES):
                    m = pe.transpose(pE[:, t * P:(t + 1) * P], src[:, (NG + 2 * t) * D:(NG + 2 * t + 2) * D], ident[:, :])
                m.then_inc(e_trans.sem, 1)

            def hidden(b):
                pe.wait_ge(e_copied.sem, e_copied.at(0, b))
                pe.wait_ge(in_keys.sem(b), in_keys.at(0, b))
                pe.matmul(pM[:, 0:TILES * P], w_h[:, :], et[b.p][:, :], start=True, stop=False)
                pe.matmul(pM[:, 0:TILES * P], w_e[:, :], attr_r[b.q][:, :], start=False, stop=True).then_inc(h_mm.sem, 1)

            def messages(ph, b):
                if ph == 0:
                    pe.wait_ge(h_act.sem, h_act.at(0, b))
                else:
                    pe.wait_ge(e_copied.sem, e_copied.at(ph, b))
                if (b - 1).real:
                    pe.wait_ge(m_act.sem, m_act.at(ph, b - 1))
                src, wt, name = [(hid, w_m0, "m0"), (et, w_nb, "nb"), (et, w_m2, "m2"), (et, w_m3, "m3")][ph]
                o = pG[:, 0, :] if ph == 0 else pM
                n = 2 * D if ph == 1 else D
                pe.matmul(o[:, 0:TILES * n], ones65[:, :], bias_of(name), start=True, stop=False)
                for t in range(TILES):
                    m = pe.matmul(o[:, t * n:(t + 1) * n], src[b.p][:, t * P:(t + 1) * P], wt[:, :],
                                  start=False, stop=(t == TILES - 1))
                m.then_inc(m_mm.sem, 1)

            def sum_by_key(ph, b):
                pe.wait_ge(m_act.sem, m_act.at(ph, b))
                pe.wait_ge(s_built.sem, s_built.at(ph, b))
                if (b - 1).real:
                    pe.wait_ge(d_act.sem, d_act.at(ph, b - 1))
                v = msg[b.p]
                if ph == 1:
                    for j in range(EG):
                        a = (j % TILES) * 2 * D + (D if j < TILES else 0)
                        m = pe.matmul(pD[:, j * D:(j + 1) * D], same[b.p][:, j, :], v[:, a:a + D], start=True, stop=True)
                else:
                    n = D + 1 if ph == 2 else D
                    for t in range(TILES):
                        m = pe.matmul(pD[:, t * n:(t + 1) * n], same[b.p][:, TILES + t, :], v[:, t * n:(t + 1) * n],
                                      start=True, stop=True)
                m.then_inc(d_mm.sem, 1)

            def body0(s):
                edge_transpose(0, s)
                hidden(s)
                messages(0, s)
                sum_by_key(0, s)

            steps(pe, body0, 0)

            for ph in range(1, 4):
                def body(s, ph=ph, f=NORM_SKEW[ph]):
                    if first(s):
                        transpose_chunk(ph, s, 0)
                        transpose_chunk(ph, s, 1)
                    if s.real:
                        update_chunk(ph, s, 0)
                        transpose_chunk(ph, s, 2)
                        update_chunk(ph, s, 1)
                    if (s - f - 1).real:
                        messages(ph, s - f - 1)
                    if (s + 1).real:
                        transpose_chunk(ph, s + 1, 0)
                    if s.real:
                        update_chunk(ph, s, 2)
                    if (s + 1).real:
                        transpose_chunk(ph, s + 1, 1)
                    if (s - f).real:
                        edge_transpose(ph, s - f)
                    if (s - f - 1).real:
                        sum_by_key(ph, s - f - 1)

                steps(pe, body, NORM_SKEW[ph] + 1, ahead=2)

            def body4(s):
                if first(s):
                    transpose_chunk(4, s, 0)
                    transpose_chunk(4, s, 1)
                update_chunk(4, s, 0)
                if (s + 1).real:
                    transpose_chunk(4, s + 1, 0)
                update_chunk(4, s, 1)
                if (s + 1).real:
                    transpose_chunk(4, s + 1, 1)

            steps(pe, body4, 0, ahead=2)

        @block.scalar
        def _(act):
            def zero_table0(at, n):
                act.dma_start(table[0].rearrange("(p k r) d -> p k (r d)", p=P, k=PAIRS // 2)[:, at:at + n, :],
                              zeros[:, :].unsqueeze(1).broadcast_to([P, n, 2 * NG * D])).then_inc(zero0, 16)

            def put(dst, src):
                act.dma_start(dst, src.unsqueeze(0).broadcast_to(list(dst.shape))).then_inc(b_landed, 16)

            act.wait_ge(ready, 1)
            zero_table0(0, ZERO_FIRST)
            act.wait_ge(ready, 2)
            put(bias[:, 0:3 * D], w["L0_b_ih"])
            put(bias_hh[:, 0:2 * D], w["L0_b_hh"][0:2 * D])
            put(bias_hh[:, 3 * D:4 * D], w["L0_b_hh"][2 * D:3 * D])
            for name, src in (("m0", "L0_b2"), ("self", "L1_w0_b"), ("nb", "L1_w1_b"), ("m2", "L2_b_msg"),
                              ("u2", "L2_b_upd"), ("m3", "L3_b_msg"), ("u3", "L3_b_upd")):
                put(bias[:, ONCE[name][0]:ONCE[name][0] + D], w[src])
            act.wait_ge(w_landed, 16 * WEIGHT_DMAS)
            act.wait_ge(b_landed, 16 * BIAS_DMAS)
            zero_table0(ZERO_FIRST, PAIRS // 2 - ZERO_FIRST)
            act.wait_ge(ready, 3)

            def copy_chunk(ph, b, k):
                act.wait_ge(t_done.sem, t_done.at(ph, b, k))
                c = buf(ph, b, k)
                if b.reg is not None or CHUNKS[ph] * b.c + k >= 2:
                    act.wait_ge(g_done.sem, g_done.at(ph, b, k - 2))
                n = min(updated[ph], (k + 1) * CH) - k * CH
                n = n * P if ph in (1, 3) else n * D
                act.copy(xt[c][:, 0:n], pT[:, c, 0:n]).then_inc(t_copied.sem, 1)

            def gate_chunk(b, k):
                act.wait_ge(g_done.sem, g_done.at(1, b, k))
                if (b - 2).real:
                    act.wait_ge(zd_done.sem, zd_done.at(1, b - 2))
                c = bank(1, b, k)
                act.activation(groups(gates[b.p], k * CH, CH, 2 * D),
                               pG[:, c:c + 2, :].rearrange("p a (g c) -> p (a g) c", c=256)[:, :, 0:2 * D],
                               ACT.Sigmoid).then_inc(gate_done.sem, 1)

            def tanh(b):
                act.wait_ge(g_used.sem, g_used.at(1, b, 2))
                if (b - 2).real:
                    act.wait_ge(diff_done.sem, diff_done.at(1, b - 2))
                act.activation(act_n[b.p][:, :], pre_n[b.p][:, :], ACT.Tanh).then_inc(tanh_done.sem, 1)

            def deviation(b):
                act.wait_ge(ssq_done.sem, ssq_done.at(2, b))
                if (b - 1).real:
                    act.wait_ge(newton.sem, newton.at(2, b - 1))
                act.activation(std[:, :], ssq[:, b.p, :], ACT.Sqrt, bias=eps_col[:, 0:1], scale=1.0 / D
                               ).then_inc(std_done.sem, 1)

            def square(ph, b):
                act.wait_ge(cen_done.sem, cen_done.at(ph, b))
                if (b - 2).real:
                    act.wait_ge(ssq_done.sem, ssq_done.at(ph, b - 2))
                n = updated[ph] * D
                act.activation(sq[b.p][:, 0:n], y[b.q][:, 0:n], ACT.Square).then_inc(sq_done.sem, 1)

            def scale(b):
                may_scale(act, 4, b)
                rinv = rinv_i[b.q // 2][:, b.p, :].bitcast(F32)
                for g in range(NG):
                    i = act.activation(groups(xn[b.q], g, 1)[:, 0, :], groups(y[b.q], g, 1)[:, 0, :], ACT.Copy,
                                       scale=rinv[:, g:g + 1])
                i.then_inc(ln_done.sem, 1)

            def copy_edges(ph, b):
                act.wait_ge(e_trans.sem, e_trans.at(ph, b))
                if (b - 2).real:
                    free = h_mm if ph == 0 else m_mm
                    act.wait_ge(free.sem, free.at(ph, b - 2))
                act.copy(et[b.p][:, :], pE[:, 0:TILES * P]).then_inc(e_copied.sem, 1)

            def act_messages(ph, b):
                act.wait_ge(m_mm.sem, m_mm.at(ph, b))
                if (b - 2).real:
                    act.wait_ge(d_mm.sem, d_mm.at(ph, b - 2))
                if ph == 2:
                    i = act.activation(groups(msg[b.p], 0, TILES, D + 1)[:, :, 0:D], groups(pM, 0, TILES), ACT.Relu)
                elif ph == 3:
                    i = act.activation(msg[b.p][:, 0:TILES * D], pM[:, 0:TILES * D], ACT.Gelu_apprx_tanh)
                elif ph == 1:
                    i = act.copy(msg[b.p][:, 0:TILES * 2 * D], pM[:, 0:TILES * 2 * D])
                else:
                    i = act.copy(msg[b.p][:, 0:TILES * D], pG[:, 0, 0:TILES * D])
                i.then_inc(m_act.sem, 1)

            def copy_sums(ph, b):
                act.wait_ge(d_mm.sem, d_mm.at(ph, b))
                if (b - SLOTS).real:
                    act.wait_ge(dst_added, dst_at(ph, b - SLOTS, 1))
                    if ph == 1:
                        act.wait_ge(src_added, src_at(b - SLOTS, 1))
                n = {0: TILES * D, 1: EG * D, 2: TILES * (D + 1), 3: TILES * D}[ph]
                act.copy(summed[b.q][:, 0:n], pD[:, 0:n]).then_inc(d_act.sem, 1)

            def body0(b):
                copy_edges(0, b)
                act.wait_ge(h_mm.sem, h_mm.at(0, b))
                if (b - 2).real:
                    act.wait_ge(m_mm.sem, m_mm.at(0, b - 2))
                act.activation(hid[b.p][:, :], pM[:, 0:TILES * P], ACT.Relu, bias=b_h[:, 0:1]).then_inc(h_act.sem, 1)
                act_messages(0, b)
                copy_sums(0, b)

            steps(act, body0, 0)

            for ph in range(1, 4):
                if ph == 2:
                    for q in two:
                        act.activation(groups(msg[q], 0, TILES, D + 1)[:, :, D:D + 1],
                                       groups(zeros, 0, TILES, D)[:, :, 0:1], ACT.Copy, bias=1.0)

                def body(s, ph=ph, f=NORM_SKEW[ph]):
                    if first(s):
                        copy_chunk(ph, s, 0)
                        copy_chunk(ph, s, 1)
                    if ph == 1 and (s - 1).real:
                        tanh(s - 1)
                    if ph == 2 and (s - 2).real:
                        deviation(s - 2)
                    if s.real:
                        if ph == 1:
                            gate_chunk(s, 0)
                        copy_chunk(ph, s, 2)
                        if ph == 1:
                            gate_chunk(s, 1)
                    if (s - f - 1).real:
                        act_messages(ph, s - f - 1)
                    if (s + 1).real:
                        copy_chunk(ph, s + 1, 0)
                    b = s - (2 if ph == 1 else 1)
                    if b.real:
                        square(ph, b)
                    if ph == 1 and s.real:
                        gate_chunk(s, 2)
                    if (s + 1).real:
                        copy_chunk(ph, s + 1, 1)
                    if (s - f).real:
                        copy_edges(ph, s - f)
                    if (s - f - 1).real:
                        copy_sums(ph, s - f - 1)

                steps(act, body, NORM_SKEW[ph] + 1, ahead=2)

            def body4(s):
                if first(s):
                    copy_chunk(4, s, 0)
                    copy_chunk(4, s, 1)
                for k in range(2):
                    if s.real:
                        act.wait_ge(g_done.sem, g_done.at(4, s, k))
                        if (s - 2).real:
                            act.wait_ge(y_done.sem, y_done.at(4, s - 2))
                        act.activation(act_n[s.p][:, k * CH * D:(k + 1) * CH * D], pG[:, bank(4, s, k), 0:CH * D],
                                       ACT.Gelu_apprx_tanh).then_inc(g_used.sem, 1)
                    if (s + 1).real:
                        copy_chunk(4, s + 1, k)
                if (s - 1).real:
                    square(4, s - 1)
                if (s - 3).real:
                    scale(s - 3)

            steps(act, body4, 3, ahead=2)

        @block.vector
        def _(dve):
            dve.memset(zeros[:, :], 0.0).then_inc(ready, 1)
            for t in (w_gru, w_self, w_nb, w_u3, bias, bias_hh, bias3):
                dve.memset(t[:, :], 0.0)
            dve.memset(eps_col[:, :], EPS)
            dve.memset(ones65[:, :], 1.0).then_inc(ready, 1)
            dve.wait_ge(pool_ready, 5)
            dve.tensor_copy(spare[:, :], spare_i[:, :])
            dve.wait_ge(w_landed, 16 * WEIGHT_DMAS)
            dve.wait_ge(b_landed, 16 * BIAS_DMAS)
            dve.tensor_tensor(w_self[:, :], w_self[:, :], ident[:, :], ALU.add).then_inc(prep_w, 1)
            dve.tensor_scalar(w_gru[:, D:2 * D], w_gru[:, D:2 * D], -1.0, None, ALU.mult).then_inc(prep_w, 1)
            dve.tensor_scalar(eps1p[:, :], eps1[:, :], 1.0, None, ALU.add).then_inc(prep_w, 1)
            dve.tensor_tensor(bias[:, 0:256], bias[:, 0:256], bias_hh[:, :], ALU.add).then_inc(prep_w, 1)
            dve.wait_ge(prep_w, 4)
            zc = bias[:, D:2 * D]
            dve.tensor_scalar(zc, zc, -1.0, None, ALU.mult).then_inc(prep_w, 1)
            dve.wait_ge(prep_w, 5)
            dve.tensor_copy(bias_hi[:, :], bias[:, :]).then_inc(prep_w, 1)
            dve.wait_ge(prep_w, 6)
            dve.tensor_tensor(bias_r1[:, :], bias[:, :], bias_hi[:, :], ALU.subtract).then_inc(prep_w, 1)
            dve.wait_ge(prep_w, 7)
            dve.tensor_copy(bias_mid[:, :], bias_r1[:, :]).then_inc(prep_w, 1)
            dve.wait_ge(prep_w, 8)
            dve.tensor_tensor(bias_r2[:, :], bias_r1[:, :], bias_mid[:, :], ALU.subtract).then_inc(prep_w, 1)
            dve.wait_ge(prep_w, 9)
            dve.tensor_copy(bias_lo[:, :], bias_r2[:, :]).then_inc(prep_w, 1)
            dve.wait_ge(prep_w, 10)
            for row, part in ((0, bias_hi), (32, bias_mid), (64, bias_lo)):
                for name, (a, m) in BIAS.items():
                    o, n = ONCE[name]
                    i = dve.tensor_copy(bias3[row:row + 1, a:a + m].rearrange("p (r c) -> p r c", c=n),
                                        part[row:row + 1, o:o + n].unsqueeze(1).broadcast_to([1, m // n, n]))
            i.then_inc(ready, 1)

            def build_same(ph, b):
                dve.wait_ge(in_keys.sem(b), in_keys.at(ph, b))
                if (b - 2).real:
                    dve.wait_ge(d_mm.sem, d_mm.at(ph, b - 2))
                a = 0 if ph < 2 else TILES
                dve.tensor_tensor(same[b.p][:, a:EG, :], groups(keyr[b.q], a, EG - a, P),
                                  keyc[b.q][:, a:EG].unsqueeze(2).broadcast_to([P, EG - a, P]), ALU.is_equal
                                  ).then_inc(s_built.sem, 1)

            def center(ph, b):
                n = updated[ph]
                dve.wait_ge(sum_done.sem, sum_done.at(ph, b))
                v = groups(y[b.q], 0, n)
                dve.scalar_tensor_tensor(v, spread(tot, n), -1.0 / D, v, ALU.mult, ALU.add).then_inc(cen_done.sem, 1)

            def row_sums(ph, b):
                dve.wait_ge(y_done.sem, y_done.at(ph, b, y_done.per[ph] - 1))
                n = updated[ph]
                dve.tensor_reduce(tot[:, 0:n], groups(y[b.q], 0, n), AX_X, ALU.add).then_inc(sum_done.sem, 1)

            def square_sums(ph, b):
                dve.wait_ge(sq_done.sem, sq_done.at(ph, b))
                n = updated[ph]
                if ph == 2 and (b - 2).real:
                    dve.wait_ge(std_done.sem, std_done.at(2, b - 2))
                dve.tensor_reduce(ssq[:, b.p, 0:n], groups(sq[b.p], 0, n), AX_X, ALU.add).then_inc(ssq_done.sem, 1)

            def newton_step(ph, b, k):
                n = updated[ph]
                last = b + 1 if ph in BATCHED else b
                if k == 0:
                    dve.wait_ge(ssq_done.sem, ssq_done.at(ph, last))
                else:
                    dve.wait_ge(newton.sem, newton.at(ph, b, k - 1))
                if k == 2 and (b - SLOTS).real:
                    dve.wait_ge(ln_done.sem, ln_done.at(ph, last - SLOTS))

                def of(t):
                    return t[:, :, 0:n] if ph in BATCHED else t[:, b.p, 0:n]

                r = of(rinv_i[b.q // 2]).bitcast(F32)
                if k == 0:
                    i = dve.tensor_scalar(of(var), of(ssq), 1.0 / D, EPS, ALU.mult, ALU.add)
                elif k == 1:
                    i = dve.tensor_scalar(of(seed), of(var).bitcast(I32), 1, None, ALU.logical_shift_right)
                elif k == 2:
                    i = dve.tensor_scalar(of(rinv_i[b.q // 2]), of(seed), -1.0, RSQRT_SEED, ALU.mult, ALU.add)
                elif k % 3 == 0:
                    i = dve.tensor_tensor(of(nt_a), r, r, ALU.mult)
                elif k % 3 == 1:
                    i = dve.scalar_tensor_tensor(of(nt_b), of(nt_a), -0.5, of(var), ALU.mult, ALU.mult)
                else:
                    i = dve.scalar_tensor_tensor(r, of(nt_b), 1.5, r, ALU.add, ALU.mult)
                i.then_inc(newton.sem, 1)

            def body0(b):
                build_same(0, b)
                if (b - SLOTS).real:
                    dve.wait_ge(st_rows.sem(b), st_rows.at(0, b - SLOTS))
                    dve.wait_ge(dst_added, dst_at(0, b - SLOTS, 1))
                dve.tensor_copy(key_f[:, :], keyc[b.q][:, :]).then_inc(prep.sem, 1)
                dve.wait_ge(s_built.sem, s_built.at(0, b))
                dve.tensor_tensor(earlier[:, :, :], same[b.p][:, :, :], before[:, :].unsqueeze(1).broadcast_to([P, EG, P]),
                                  ALU.mult).then_inc(prep.sem, 1)
                dve.wait_ge(prep.sem, prep.at(0, b, 1))
                dve.tensor_reduce(dup[:, :], earlier[:, :, :], AX_X, ALU.add).then_inc(prep.sem, 1)
                dve.tensor_tensor(off[:, :], spare[:, :], key_f[:, :], ALU.subtract).then_inc(prep.sem, 1)
                dve.wait_ge(prep.sem, prep.at(0, b, 3))
                dve.tensor_scalar(dup1[:, :], dup[:, :], 1.0, None, ALU.min).then_inc(prep.sem, 1)
                dve.wait_ge(prep.sem, prep.at(0, b, 4))
                dve.tensor_tensor(off1[:, :], off[:, :], dup1[:, :], ALU.mult).then_inc(prep.sem, 1)
                dve.wait_ge(prep.sem, prep.at(0, b, 5))
                dve.tensor_tensor(row_f[:, :], off1[:, :], key_f[:, :], ALU.add).then_inc(prep.sem, 1)
                dve.wait_ge(prep.sem, prep.at(0, b, 6))
                dve.tensor_copy(s_rows[b.q][:, 0:EG], row_f[:, :]).then_inc(prep.sem, 1)
                dve.tensor_scalar(s_rows[b.q][:, EG:EG + TILES], row_f[:, 0:TILES], 2.0, 1.0, ALU.mult, ALU.add
                                  ).then_inc(prep.sem, 1)
                dve.tensor_scalar(s_rows[b.q][:, EG + TILES:2 * EG], row_f[:, TILES:EG], 2.0, None, ALU.mult
                                  ).then_inc(prep.sem, 1)

            steps(dve, body0, 0)

            def scale(ph, b):
                if not b.real:
                    return
                may_scale(dve, ph, b)
                n = updated[ph]
                rinv = rinv_i[b.q // 2][:, b.p, :].bitcast(F32)
                m = NG if ph == 3 else n
                i = dve.tensor_tensor(groups(xn[b.q], 0, m), groups(y[b.q], 0, m), spread(rinv, m), ALU.mult)
                if ph == 3:
                    i = dve.tensor_tensor(groups(xn[b.q], NG, EG)[:, 0:EG:2, :], groups(y[b.q], NG, TILES),
                                          rinv[:, NG:n].unsqueeze(2).broadcast_to([P, TILES, D]), ALU.mult)
                i.then_inc(ln_done.sem, 1)

            def times_r(b, k):
                dve.wait_ge(gate_done.sem, gate_done.at(1, b, k))
                if (b - 2).real:
                    dve.wait_ge(tanh_done.sem, tanh_done.at(1, b - 2))
                c = bank(1, b, k)
                g = pG[:, c:c + 2, :].rearrange("p a (g c) -> p (a g) c", c=256)
                dve.tensor_tensor(groups(pre_n[b.p], k * CH, CH), groups(gates[b.p], k * CH, CH, 2 * D)[:, :, 0:D],
                                  g[:, :, 3 * D:4 * D], ALU.mult).then_inc(rn_done.sem, 1)

            def plus_n(b, k):
                dve.wait_ge(rn_done.sem, rn_done.at(1, b, k))
                c = bank(1, b, k)
                g = pG[:, c:c + 2, :].rearrange("p a (g c) -> p (a g) c", c=256)
                v = groups(pre_n[b.p], k * CH, CH)
                dve.tensor_tensor(v, v, g[:, :, 2 * D:3 * D], ALU.add).then_inc(g_used.sem, 1)

            def y_free(ph, b):
                if (b - SLOTS).real:
                    dve.wait_ge(ln_done.sem, ln_done.at(ph, b - SLOTS))

            def newton_steps(ph, b, first, last):
                if b.real and not (ph in BATCHED and b.p):
                    for k in range(first, last):
                        newton_step(ph, b, k)

            def body1(s):
                h, f, m = s - 1, s - 2, s - 4
                if s.real:
                    times_r(s, 0)
                newton_steps(1, m, 0, 1)
                if s.real:
                    times_r(s, 1)
                newton_steps(1, m, 1, 2)
                if s.real:
                    plus_n(s, 0)
                newton_steps(1, m, 2, 3)
                if s.real:
                    plus_n(s, 1)
                newton_steps(1, m, 3, 4)
                if h.real:
                    dve.wait_ge(tanh_done.sem, tanh_done.at(1, h))
                    dve.wait_ge(in_rows.sem(h), in_rows.at(1, h))
                    dve.tensor_tensor(groups(diff[h.p], 0, G), groups(act_n[h.p], 0, G), x_of(1, h, 0, G), ALU.subtract
                                      ).then_inc(diff_done.sem, 1)
                newton_steps(1, m, 4, 5)
                if h.real:
                    dve.wait_ge(diff_done.sem, diff_done.at(1, h))
                    dve.tensor_tensor(groups(diff[h.p], 0, G), groups(gates[h.p], 0, G, 2 * D)[:, :, D:2 * D],
                                      groups(diff[h.p], 0, G), ALU.mult).then_inc(zd_done.sem, 1)
                newton_steps(1, m, 5, 6)
                if h.real:
                    dve.wait_ge(zd_done.sem, zd_done.at(1, h))
                    y_free(1, h)
                    dve.scalar_tensor_tensor(groups(y[h.q], 0, G), x_of(1, h, 0, G), 2.0, groups(diff[h.p], 0, G), ALU.mult, ALU.add
                                             ).then_inc(y_done.sem, 1)
                newton_steps(1, m, 6, 7)
                if s.real:
                    times_r(s, 2)
                newton_steps(1, m, 7, 8)
                if s.real:
                    plus_n(s, 2)
                newton_steps(1, m, 8, 9)
                if f.real:
                    square_sums(1, f)
                newton_steps(1, m, 9, 10)
                if h.real:
                    row_sums(1, h)
                newton_steps(1, m, 10, 11)
                if (s - 5).real:
                    build_same(1, s - 5)
                newton_steps(1, m, 11, 12)
                if h.real:
                    center(1, h)
                scale(1, m)

            steps(dve, body1, 5)

            def add_first(b, k):
                dve.wait_ge(g_done.sem, g_done.at(2, b, k))
                sums = sums_of(2, b, k * CH, CH)
                dve.tensor_tensor(groups(diff[b.p], k * CH, CH), groups(pG[:, bank(2, b, k), :], 0, CH), sums[:, :, 0:D],
                                  ALU.add).then_inc(g_used.sem, 1)

            def body2(s):
                f = s - 1
                if s.real:
                    add_first(s, 0)
                    add_first(s, 1)
                if (s - 3).real:
                    build_same(2, s - 3)
                if s.real:
                    dve.wait_ge(gathered.sem(s), gathered.at(2, s))
                    add_first(s, 2)
                if (s - 2).real:
                    dve.wait_ge(std_done.sem, std_done.at(2, s - 2))
                    if (s - 4).real:
                        dve.wait_ge(ln_done.sem, ln_done.at(2, s - 4))
                    dve.reciprocal(rinv_i[(s - 2).q // 2][:, s.p, :].bitcast(F32), std[:, :]).then_inc(newton.sem, 1)
                if s.real:
                    dve.wait_ge(g_used.sem, g_used.at(2, s, 2))
                    y_free(2, s)
                    dve.tensor_tensor(groups(y[s.q], 0, G), groups(diff[s.p], 0, G),
                                      sums_of(2, s, 0, G)[:, :, D:2 * D], ALU.add).then_inc(y_done.sem, 1)
                if f.real:
                    square_sums(2, f)
                if s.real:
                    row_sums(2, s)
                scale(2, s - 2)
                if s.real:
                    center(2, s)

            steps(dve, body2, 3)

            def means(b, m=None):
                n = updated[3]
                dve.wait_ge(in_rows.sem(b), in_rows.at(3, b))
                dve.wait_ge(gathered.sem(b), gathered.at(3, b))
                sums = sums_of(3, b, 0, n)
                dve.tensor_scalar(cnt[:, 0:n].unsqueeze(2), sums[:, :, D:D + 1], 1.0, None, ALU.max).then_inc(cnt_done.sem, 1)
                if m is not None:
                    newton_steps(3, m, 4, 5)
                dve.wait_ge(cnt_done.sem, cnt_done.at(3, b, 0))
                dve.reciprocal(rcnt[:, 0:n], cnt[:, 0:n]).then_inc(cnt_done.sem, 1)
                if m is not None:
                    newton_steps(3, m, 5, 6)
                dve.wait_ge(cnt_done.sem, cnt_done.at(3, b, 1))
                dve.tensor_tensor(groups(rows[b.q], 0, n, 2 * D)[:, :, D:2 * D], sums[:, :, 0:D], spread(rcnt, n), ALU.mult
                                  ).then_inc(pre_done.sem, 1)

            def relu_plus_x(b, k):
                dve.wait_ge(g_done.sem, g_done.at(3, b, k))
                n = min(updated[3], (k + 1) * CH) - k * CH
                dve.scalar_tensor_tensor(groups(y[b.q], k * CH, n), groups(pG[:, bank(3, b, k), :], 0, n), 0.0,
                                         x_of(3, b, k * CH, n), ALU.max, ALU.add).then_inc(y_done.sem, 1)

            def body3(s):
                f, m = s - 1, s - 3
                if first(s):
                    means(s)
                    means(s + 1)
                newton_steps(3, m, 0, 1)
                for k in range(3):
                    if s.real:
                        if k == 0:
                            y_free(3, s)
                        relu_plus_x(s, k)
                    newton_steps(3, m, k + 1, k + 2)
                if (s + 2).real:
                    means(s + 2, m)
                else:
                    newton_steps(3, m, 4, 6)
                newton_steps(3, m, 6, 7)
                if s.real:
                    row_sums(3, s)
                newton_steps(3, m, 7, 8)
                if (s - 5).real:
                    build_same(3, s - 5)
                newton_steps(3, m, 8, 9)
                if s.real:
                    center(3, s)
                newton_steps(3, m, 9, 10)
                newton_steps(3, m, 10, 11)
                if f.real:
                    square_sums(3, f)
                newton_steps(3, m, 11, 12)
                scale(3, m)

            steps(dve, body3, 5, ahead=3)

            def eps_x_plus_sums(b):
                dve.wait_ge(in_rows.sem(b), in_rows.at(4, b))
                r = rows[b.q]
                dve.scalar_tensor_tensor(r[:, W:W + NG * D], r[:, 0:NG * D], eps1p[:, 0:1],
                                         r[:, RAW:RAW + NG * D], ALU.mult, ALU.add).then_inc(pre_done.sem, 1)

            def body4(s):
                f, m = s - 1, s - 2
                if first(s):
                    eps_x_plus_sums(s)
                    eps_x_plus_sums(s + 1)
                newton_steps(4, m, 0, 2)
                if (s + 2).real:
                    eps_x_plus_sums(s + 2)
                newton_steps(4, m, 2, 5)
                if f.real:
                    square_sums(4, f)
                newton_steps(4, m, 5, 8)
                if s.real:
                    row_sums(4, s)
                newton_steps(4, m, 8, 10)
                if s.real:
                    center(4, s)
                newton_steps(4, m, 10, 12)

            steps(dve, body4, 2, ahead=3)


def kernel(**inputs):
    import numpy as np
    import concourse.bacc as bacc
    from concourse.bass_utils import run_bass_kernel_spmd

    a = {k: np.asarray(v) for k, v in inputs.items()}
    slots = PAIRS * TILES

    def by_tile(v, pad):
        full = np.full((P * slots,) + v.shape[1:], pad, v.dtype)
        full[:E] = v
        return full.reshape((P, PAIRS, TILES) + v.shape[1:])

    def both(pad):
        ends = np.stack([by_tile(a["src"], pad), by_tile(a["dst"], pad)], axis=2)
        return np.ascontiguousarray(ends.transpose(1, 0, 2, 3).reshape(PAIRS, P, EG))

    arrays = {
        "x": a["x"],
        "gather_rows": both(0),
        "key_cols": both(N),
        "key_rows": np.ascontiguousarray(both(N).transpose(0, 2, 1).reshape(PAIRS, EG * P)),
        "attr_rows": np.ascontiguousarray(
            by_tile(a["edge_weight1"][:, 0], 0).transpose(1, 2, 0).reshape(PAIRS, TILES * P)),
        "attr64": by_tile(a["edge_attr_64"], 0).reshape(P, PAIRS, TILES * D),
    }
    turned = ("L0_gnn_W1", "L0_gnn_W2", "L0_gnn_W_ih", "L0_gnn_W_hh", "L1_gnn_w0_w", "L1_gnn_w1_w")
    for k, v in a.items():
        if k.startswith("L"):
            arrays[k.replace("_gnn", "")] = np.ascontiguousarray(v.T) if k in turned else v

    nc = bacc.Bacc("TRN2", target_bir_lowering=False, num_devices=1)
    t = {k: nc.dram_tensor(k, v.shape, mybir.dt.from_np(v.dtype), kind="ExternalInput").ap() for k, v in arrays.items()}
    out = nc.dram_tensor("new_x", (N, D), F32, kind="ExternalOutput").ap()
    build(nc, t["x"], t["gather_rows"], t["key_cols"], t["key_rows"], t["attr_rows"], t["attr64"], t, out)
    r = run_bass_kernel_spmd(nc, [arrays], core_ids=[0])
    return r.results[0]["new_x"]
```
